# Optimizing a Trainium2 kernel written in Bass

```python
import numpy as np
import jax
import jax.numpy as jnp

def _softmax(x, axis=-1):
    return jax.nn.softmax(x, axis=axis)

def _gelu(x):
    return jax.nn.gelu(x, approximate=True)

def _silu(x):
    return jax.nn.silu(x)

def _sigmoid(x):
    return jax.nn.sigmoid(x)

def _layernorm(x, axis=-1, eps=1e-05):
    m = jnp.mean(x, axis=axis, keepdims=True)
    v = jnp.var(x, axis=axis, keepdims=True)
    return (x - m) / jnp.sqrt(v + eps)

def _scatter_add(tgt, idx, src, axis=0):
    return tgt.at[idx].add(src)

def _segment_sum(src, seg, n):
    return jax.ops.segment_sum(src, seg, n)
kernel_name = 'mk_adj_ffn_d1_adj_r2_bb6f85'

def setup_inputs(seed: int=0):
    np.random.seed(seed)
    _w = jnp.asarray

    def _rec_inputs():
        import jax
        import jax.numpy as jnp
        _gk = jax.random.key(seed)
        x = -0.0002928 + 1 * jax.random.normal(jax.random.fold_in(_gk, 1), (8, 1024, 128), jnp.float32)
        _w = (1.0 + jnp.arange(1024, dtype=jnp.float32)) ** (-0.5)
        _w = _w / _w.mean()
        _pij = jnp.clip(0.00195312 * _w[:, None] * _w[None, :], 0.0, 1.0)
        _a = jax.random.uniform(jax.random.fold_in(_gk, 2), (8, 1024, 1024)) < _pij
        adj = _a.astype(jnp.int32)
        return (x, adj)
    x, adj = _rec_inputs()

    def _L0_gnn_setup():
        import jax, jax.numpy as jnp
        import numpy as np
        UNITS = 128
        NUM_HEADS = 8
        HEAD_DIM = UNITS // NUM_HEADS
        B, N = (8, 1024)
        key = jax.random.key(seed)
        ks = jax.random.split(key, 7)
        node_features = jax.random.normal(ks[0], (B, N, UNITS), dtype=jnp.float32)
        adjacency_matrix = jax.random.randint(ks[1], (B, N, N), 0, 2, dtype=jnp.int32)
        s = 1.0 / np.sqrt(UNITS)
        Wq = jax.random.normal(ks[2], (UNITS, UNITS), dtype=jnp.float32) * s
        Wk = jax.random.normal(ks[3], (UNITS, UNITS), dtype=jnp.float32) * s
        Wv = jax.random.normal(ks[4], (UNITS, UNITS), dtype=jnp.float32) * s
        Wo = jax.random.normal(ks[5], (UNITS, UNITS), dtype=jnp.float32) * s
        bo = jnp.zeros((UNITS,), dtype=jnp.float32)
        return {'node_features': node_features, 'adjacency_matrix': adjacency_matrix, 'Wq': Wq, 'Wk': Wk, 'Wv': Wv, 'Wo': Wo, 'bo': bo}
    _L0_gnn_all = _L0_gnn_setup()
    _L0_gnn_in = {k: v for k, v in _L0_gnn_all.items() if k in ('Wq', 'Wk', 'Wv', 'Wo', 'bo')}
    del _L0_gnn_all

    def _L0_ffn_setup():
        import jax, jax.numpy as jnp
        import numpy as np
        D_MODEL = 128
        N_EXPERTS = 16
        HIDDEN = 256
        SCALE = 0.02
        key = jax.random.key(seed)
        ks = jax.random.split(key, 5)
        x = jax.random.normal(ks[0], (4, 4096, D_MODEL), dtype=jnp.float32)
        gate_w = jax.random.normal(ks[1], (D_MODEL, N_EXPERTS), dtype=jnp.float32) * SCALE
        gate_b = jnp.zeros((N_EXPERTS,), dtype=jnp.float32)
        w1 = jax.random.normal(ks[2], (N_EXPERTS, D_MODEL, HIDDEN), dtype=jnp.float32) * SCALE
        w2 = jax.random.normal(ks[3], (N_EXPERTS, D_MODEL, HIDDEN), dtype=jnp.float32) * SCALE
        w3 = jax.random.normal(ks[4], (N_EXPERTS, HIDDEN, D_MODEL), dtype=jnp.float32) * SCALE
        return {'x': x, 'gate_w': gate_w, 'gate_b': gate_b, 'w1': w1, 'w2': w2, 'w3': w3}
    _L0_ffn_all = _L0_ffn_setup()
    _L0_ffn_in = {k: v for k, v in _L0_ffn_all.items() if k in ('gate_w', 'gate_b', 'w1', 'w2', 'w3')}
    del _L0_ffn_all
    return {'x': x, 'adj': adj, 'L0_gnn_Wq': _L0_gnn_in['Wq'], 'L0_gnn_Wk': _L0_gnn_in['Wk'], 'L0_gnn_Wv': _L0_gnn_in['Wv'], 'L0_gnn_Wo': _L0_gnn_in['Wo'], 'L0_gnn_bo': _L0_gnn_in['bo'], 'L0_ffn_gate_w': _L0_ffn_in['gate_w'], 'L0_ffn_gate_b': _L0_ffn_in['gate_b'], 'L0_ffn_w1': _L0_ffn_in['w1'], 'L0_ffn_w2': _L0_ffn_in['w2'], 'L0_ffn_w3': _L0_ffn_in['w3']}

def reference(x, adj, L0_gnn_Wq, L0_gnn_Wk, L0_gnn_Wv, L0_gnn_Wo, L0_gnn_bo, L0_ffn_gate_w, L0_ffn_gate_b, L0_ffn_w1, L0_ffn_w2, L0_ffn_w3):
    import jax
    import jax.numpy as jnp

    def _L0_gnn_ref(node_features, adjacency_matrix, Wq, Wk, Wv, Wo, bo):
        import jax, jax.numpy as jnp
        import numpy as np
        UNITS = 128
        NUM_HEADS = 8
        HEAD_DIM = UNITS // NUM_HEADS
        B, N = (8, 1024)
        b, n, _ = node_features.shape
        h, d = (NUM_HEADS, HEAD_DIM)
        q = (node_features @ Wq).reshape(b, n, h, d).transpose(0, 2, 1, 3)
        k = (node_features @ Wk).reshape(b, n, h, d).transpose(0, 2, 1, 3)
        v = (node_features @ Wv).reshape(b, n, h, d).transpose(0, 2, 1, 3)
        scores = jnp.einsum('bhqd,bhkd->bhqk', q, k) / jnp.sqrt(jnp.float32(d))
        mask = adjacency_matrix[:, None, :, :] > 0
        scores = jnp.where(mask, scores, jnp.float32(-1000000000.0))
        w = jax.nn.softmax(scores, axis=-1)
        ctx = jnp.einsum('bhqk,bhkd->bhqd', w, v)
        ctx = ctx.transpose(0, 2, 1, 3).reshape(b, n, h * d)
        return ctx @ Wo + bo

    def _L0_ffn_ref(x, gate_w, gate_b, w1, w2, w3):
        import jax, jax.numpy as jnp
        import numpy as np
        D_MODEL = 128
        N_EXPERTS = 16
        HIDDEN = 256
        SCALE = 0.02
        n_experts = w1.shape[0]
        logits = jnp.einsum('bsd,de->bse', x, gate_w) + gate_b
        probs = jax.nn.softmax(logits, axis=-1)
        top_probs, top_idx = jax.lax.top_k(probs, 2)
        top_probs = top_probs / jnp.sum(top_probs, axis=-1, keepdims=True)
        dispatch = jnp.sum(jax.nn.one_hot(top_idx, n_experts, dtype=x.dtype) * top_probs[..., None], axis=-2)
        h1 = jnp.einsum('bsd,edh->bseh', x, w1)
        h2 = jnp.einsum('bsd,edh->bseh', x, w2)
        hidden = jax.nn.silu(h1) * h2
        expert_out = jnp.einsum('bseh,eho->bseo', hidden, w3)
        return jnp.einsum('bseo,bse->bso', expert_out, dispatch)
    x = x + _L0_gnn_ref(_layernorm(x, axis=-1), adj, L0_gnn_Wq, L0_gnn_Wk, L0_gnn_Wv, L0_gnn_Wo, L0_gnn_bo)
    x = x + _L0_ffn_ref(_layernorm(x, axis=-1), L0_ffn_gate_w, L0_ffn_gate_b, L0_ffn_w1, L0_ffn_w2, L0_ffn_w3)
    return x

_drawn_inputs = setup_inputs


def setup_inputs(seed=0):
    import zlib

    import numpy as np

    out = dict(_drawn_inputs(seed))
    spreads = {'L0_gnn_bo': (0.0, 0.1), 'L0_ffn_gate_b': (0.0, 0.8)}
    factors = {'L0_ffn_gate_w': 8.0, 'L0_ffn_w1': 8.0, 'L0_ffn_w2': 8.0, 'L0_ffn_w3': 8.0}
    for name, (base, spread) in spreads.items():
        noise = np.random.default_rng([zlib.crc32(name.encode()), seed]).standard_normal(out[name].shape)
        drawn = base * np.exp(spread * noise) if base else spread * noise
        out[name] = jnp.asarray(drawn.astype(out[name].dtype))
    for name, factor in factors.items():
        out[name] = (out[name] * factor).astype(out[name].dtype)
    return out
```

```python
from contextlib import ExitStack

import concourse.bass as bass
from concourse import mybir

F32 = mybir.dt.float32
BF16 = mybir.dt.bfloat16
I32 = mybir.dt.int32
ALU = mybir.AluOpType
ACT = mybir.ActivationFunctionType

P = 128
B, N, D = 8, 1024, 128
H, HD = 8, 16
TOKENS = B * N
TILES = TOKENS // P
TPB = N // P
E, HID = 16, 256
EPS = 1e-5
SCALE = HD ** -0.5

Q_BLOCKS = (0, 0, 1, 1, 0, 2)
K_BLOCKS = (0, 1, 0, 1, 2, 0)
SROWS = HD * len(Q_BLOCKS)
MROWS = 3 * H
AROWS = SROWS + MROWS
HALF = 512
HALVES = TOKENS // HALF
QPH = HALF // P
HPG = 4
GROUPS = H // HPG
VW = 32
MASKED = -2.0 ** 100


def prepare(nc, t, x, wq, wk, wv):
    x_v = x.rearrange("b (t p) d -> b p t d", p=P)
    ctx = ExitStack()
    with ctx:
        sb = lambda name, shape, dt=F32: ctx.enter_context(nc.sbuf_tensor(name, shape, dt))
        sem = lambda name: ctx.enter_context(nc.semaphore(name))
        two = lambda name: [sem(f"{name}{p}") for p in range(2)]
        w_in = [sb(f"w_in{k}", [P, D]) for k in range(3)]
        xin = [sb(f"xin{p}", [P, TPB, D]) for p in range(2)]
        xn = [sb(f"xn{p}", [P, TPB, D]) for p in range(2)]
        xnT = [sb(f"xnT{p}", [P, N]) for p in range(2)]
        stats = [sb(f"stats{p}", [P, TPB, 6]) for p in range(2)]
        meanvar = [sb(f"meanvar{p}", [P, TPB, 2]) for p in range(2)]
        vareps = [sb(f"vareps{p}", [P, TPB]) for p in range(2)]
        std = [sb(f"std{p}", [P, TPB]) for p in range(2)]
        rstd = [sb(f"rstd{p}", [P, TPB]) for p in range(2)]
        qk32 = [sb(f"qk32{p}", [P, 2, N]) for p in range(2)]
        rest = [sb(f"rest{p}", [P, 2, N]) for p in range(2)]
        parts = [sb(f"parts{p}", [P, 2, 3, N], BF16) for p in range(2)]
        vpad = [sb(f"vpad{p}", [P, TPB, H, VW]) for p in range(2)]
        xT_ps = [ctx.enter_context(nc.psum_tensor(f"xT_ps{p}", [P, N], F32)) for p in range(2)]
        out_ps = ctx.enter_context(nc.psum_tensor("out_ps", [P, 4, HALF], F32))
        w_loaded, x_loaded = sem("w_loaded"), two("x_loaded")
        stat_done, aggr_done, vareps_done = two("stat_done"), two("aggr_done"), two("vareps_done")
        std_done, rstd_done, xn_done = two("std_done"), two("rstd_done"), two("xn_done")
        xT_done, xnT_done = two("xT_done"), two("xnT_done")
        chunk_done, chunk_free = sem("chunk_done"), sem("chunk_free")
        hi_done, rest_done, mid_done, lo_done = two("hi_done"), two("rest_done"), two("mid_done"), two("lo_done")
        v_done, parts_stored, v_stored, pad_done = two("v_done"), two("parts_stored"), two("v_stored"), sem("pad_done")
        CH = 6
        block = ctx.enter_context(nc.Block())

        @block.sync
        def _(sp):
            for k, w in enumerate((wq, wk, wv)):
                sp.dma_start(w_in[k][:, :], w).then_inc(w_loaded, 16)
            with sp.Fori(0, B // 2) as i:
                for p in range(2):
                    sp.wait_ge(xn_done[p], TPB * i)
                    sp.dma_start(xin[p][:, :, :], x_v[2 * i + p]).then_inc(x_loaded[p], 16)

        @block.vector
        def _(dve):
            for p in range(2):
                dve.memset(vpad[p][:, :, :, HD:HD + 1], 1.0).then_inc(pad_done, 1)
                dve.memset(vpad[p][:, :, :, HD + 1:VW], 0.0).then_inc(pad_done, 1)
            with dve.Fori(0, B // 2) as i:
                for p in range(2):
                    dve.wait_ge(x_loaded[p], 16 * i + 16)
                    for t_ in range(TPB):
                        nc.vector.bn_stats(stats[p][:, t_, :], xin[p][:, t_, :]).then_inc(stat_done[p], 1)
                    for t_ in range(TPB):
                        dve.wait_ge(stat_done[p], TPB * i + t_ + 1)
                        t.alone(dve)
                        nc.vector.bn_aggr(meanvar[p][:, t_, :], stats[p][:, t_, :]).then_inc(aggr_done[p], 1)
                    dve.wait_ge(aggr_done[p], TPB * i + TPB)
                    nc.vector.tensor_scalar(vareps[p][:, :], meanvar[p][:, :, 1], EPS, None, ALU.add)\
                        .then_inc(vareps_done[p], 1)
                for p in range(2):
                    dve.wait_ge(std_done[p], i + 1)
                    nc.vector.reciprocal(rstd[p][:, :], std[p][:, :]).then_inc(rstd_done[p], 1)
                    dve.wait_ge(rstd_done[p], i + 1)
                    dve.wait_ge(xT_done[p], i)
                    for t_ in range(TPB):
                        nc.vector.tensor_scalar(xn[p][:, t_, :], xin[p][:, t_, :], meanvar[p][:, t_, 0:1],
                                                rstd[p][:, t_:t_ + 1], ALU.subtract, ALU.mult)\
                            .then_inc(xn_done[p], 1)
                for p in range(2):
                    for k in range(2):
                        dve.wait_ge(hi_done[p], 2 * i + k + 1)
                        dve.wait_ge(lo_done[p], 2 * i)
                        nc.vector.tensor_tensor(rest[p][:, k, :], qk32[p][:, k, :], parts[p][:, k, 0, :],
                                                ALU.subtract).then_inc(rest_done[p], 1)
                    for k in range(2):
                        dve.wait_ge(rest_done[p], 2 * i + k + 1)
                        nc.vector.tensor_copy(parts[p][:, k, 1, :], rest[p][:, k, :]).then_inc(mid_done[p], 1)

        @block.tensor
        def _(pe):
            pe.wait_ge(w_loaded, 48)
            pe.wait_ge(t.consts_done, t.CONSTS)
            with pe.Fori(0, B // 2) as i:
                for p in range(2):
                    pe.wait_ge(xnT_done[p], i)
                    for t_ in range(TPB):
                        pe.wait_ge(xn_done[p], TPB * i + t_ + 1)
                        last = nc.tensor.transpose(xT_ps[p][:, t_ * P:(t_ + 1) * P], xn[p][:, t_, :], t.ident[:, :])
                    last.then_inc(xT_done[p], 1)
                for p in range(2):
                    pe.wait_ge(xnT_done[p], i + 1)
                    for c in range(CH):
                        at = CH * p + c
                        if at >= 4:
                            pe.wait_ge(chunk_free, 2 * CH * i + at - 3)
                        else:
                            pe.wait_ge(chunk_free, 2 * CH * i)
                        bank, half = out_ps[:, at % 4, :], c % 2
                        if c < 4:
                            last = nc.tensor.matmul(bank, w_in[c // 2][:, :], xnT[p][:, half * HALF:(half + 1) * HALF],
                                                    start=True, stop=True)
                        else:
                            for j in range(QPH):
                                tok = (half * QPH + j) * P
                                last = nc.tensor.matmul(bank[:, j * P:(j + 1) * P], xnT[p][:, tok:tok + P], w_in[2][:, :],
                                                        start=True, stop=True)
                        last.then_inc(chunk_done, 1)

        @block.scalar
        def _(act):
            act.wait_ge(pad_done, 4)
            with act.Fori(0, B // 2) as i:
                for p in range(2):
                    act.wait_ge(vareps_done[p], i + 1)
                    nc.scalar.activation(std[p][:, :], vareps[p][:, :], ACT.Sqrt).then_inc(std_done[p], 1)
                for p in range(2):
                    act.wait_ge(xT_done[p], i + 1)
                    act.wait_ge(chunk_done, 2 * CH * i)
                    nc.scalar.activation(xnT[p][:, :], xT_ps[p][:, :], ACT.Copy).then_inc(xnT_done[p], 1)
                for p in range(2):
                    act.wait_ge(rest_done[p], 2 * i)
                    act.wait_ge(v_stored[p], 16 * i)
                    for c in range(CH):
                        act.wait_ge(chunk_done, 2 * CH * i + CH * p + c + 1)
                        bank, half = out_ps[:, (CH * p + c) % 4, :], c % 2
                        if c < 4:
                            nc.scalar.activation(qk32[p][:, c // 2, half * HALF:(half + 1) * HALF], bank, ACT.Copy)\
                                .then_inc(chunk_free, 1)
                        else:
                            src = bank.rearrange("p (t h d) -> p t h d", h=H, d=HD)
                            nc.scalar.activation(vpad[p][:, half * QPH:(half + 1) * QPH, :, 0:HD], src, ACT.Copy)\
                                .then_inc(chunk_free, 1)
                    act.wait_ge(parts_stored[p], 16 * i)
                    act.wait_ge(chunk_free, 2 * CH * i + CH * (p + 1))
                    for k in range(2):
                        nc.scalar.activation(parts[p][:, k, 0, :], qk32[p][:, k, :], ACT.Copy).then_inc(hi_done[p], 1)

        @block.gpsimd
        def _(pool):
            with pool.Fori(0, B // 2) as i:
                for p in range(2):
                    pool.wait_ge(chunk_free, 2 * CH * i + CH * (p + 1))
                    pool.dma_start(t.v_dram[2 * i + p].rearrange("(t p) c -> p t c", p=P),
                                   vpad[p][:, :, :, :].rearrange("p t h w -> p t (h w)")).then_inc(v_stored[p], 16)
                    for k in range(2):
                        pool.wait_ge(mid_done[p], 2 * i + k + 1)
                        nc.gpsimd.tensor_tensor(parts[p][:, k, 2, :], rest[p][:, k, :], parts[p][:, k, 1, :],
                                                ALU.subtract).then_inc(lo_done[p], 1)
                    pool.wait_ge(lo_done[p], 2 * i + 2)
                    pool.dma_start(t.parts_dram[2 * i + p].rearrange("w s p n -> p w s n"), parts[p][:, :, :, :])\
                        .then_inc(parts_stored[p], 16)
            for p in range(2):
                pool.wait_ge(v_stored[p], 16 * (B // 2))
                pool.wait_ge(parts_stored[p], 16 * (B // 2))


def attention(nc, t, adj):
    adj_v = adj.rearrange("b (t p) k -> b t p k", p=P)
    ctx = ExitStack()
    with ctx:
        sb = lambda name, shape, dt=F32: ctx.enter_context(nc.sbuf_tensor(name, shape, dt))
        ps = lambda name, shape, dt=F32: ctx.enter_context(nc.psum_tensor(name, shape, dt))
        sem = lambda name: ctx.enter_context(nc.semaphore(name))
        ADJ_RING, ST_RING, P_RING, S1 = 4, 3, 8, 2
        qpack = sb("qpack", [P, 2, H, N], BF16)
        kpack = sb("kpack", [P, 2, H, N], BF16)
        mask1 = sb("mask1", [P, QPH, N], BF16)
        mask2 = sb("mask2", [P, 2, QPH, N], BF16)
        adj_in = sb("adj_in", [P, ADJ_RING, N], I32)
        vbuf = [sb(f"vbuf{g}", [P, TPB, HPG, VW]) for g in range(GROUPS)]
        probs = sb("probs", [P, P_RING, HALF])
        dump = sb("dump", [P, 2, N], BF16)
        rowmax = sb("rowmax", [P, QPH, H])
        negmax_rest = sb("negmax_rest", [P, QPH, H])
        negmax = sb("negmax", [P, QPH, 3, H], BF16)
        ctx_sb = sb("ctx_sb", [P, GROUPS, HALF])
        s1_ps = ps("s1_ps", [P, S1, N])
        st_ps = ps("st_ps", [P, ST_RING, HALF])
        pv_ps = ps("pv_ps", [P, HALF])
        sel = sb("sel", [P, H], BF16)
        sel_step, sel_placed = sem("sel_step"), sem("sel_placed")
        packs_loaded = sem("packs_loaded")
        adj_loaded = [sem(f"adj_loaded{r}") for r in range(ADJ_RING)]
        v_loaded = [sem(f"v_loaded{g}") for g in range(GROUPS)]
        mask_done, mask2_done, s1_done, s1_free = sem("mask_done"), sem("mask2_done"), sem("s1_done"), sem("s1_free")
        neg_step, negT_done, neg_placed = sem("neg_step"), sem("negT_done"), sem("neg_placed")
        st_done, exp_done, pv_done, ctx_done = sem("st_done"), sem("exp_done"), sem("pv_done"), sem("ctx_done")
        ctx_stored = [sem(f"ctx_stored{g}") for g in range(GROUPS)]
        U1 = QPH * H
        STEPS = GROUPS * TPB
        U2 = STEPS * HPG
        S1_PER_STEP = 3
        NEG_AT = -(-U1 // S1_PER_STEP) + 1
        LOADS = 2 * len(Q_BLOCKS)
        block = ctx.enter_context(nc.Block())

        @block.sync
        def _(sp):
            def load_graph(b, waits):
                if waits:
                    sp.wait_ge(packs_loaded, 16 * LOADS * b)
                    t.alone(sp)
                    sp.wait_ge(st_done, 2 * U2 * (b - 1))
                for pack, w, blocks in ((qpack, 0, Q_BLOCKS), (kpack, 1, K_BLOCKS)):
                    for j, part in enumerate(blocks):
                        sp.dma_start(pack[j * HD:(j + 1) * HD, b % 2, :, :],
                                     t.parts_dram[b, w, part].rearrange("(h d) n -> d h n", d=HD))\
                            .then_inc(packs_loaded, 16)
                for qt in range(TPB):
                    if waits or qt >= ADJ_RING:
                        sp.wait_ge(mask_done, TPB * b + qt - ADJ_RING + 1)
                    sp.dma_start(adj_in[:, qt % ADJ_RING, :], adj_v[b, qt]).then_inc(adj_loaded[qt % ADJ_RING], 16)

            load_graph(0, False)
            with sp.Fori(1, B) as b:
                load_graph(b, True)

        @block.gpsimd
        def _(pool):
            def make_masks(n, first):
                for q in range(QPH):
                    pool.wait_ge(adj_loaded[q], 16 * n + 16)
                    if first < 1:
                        pool.wait_ge(mask2_done, QPH * (n - 1) + q + 1)
                        pool.wait_ge(s1_free, U1 * (n - 1) + H * (q + 1))
                    t.alone(pool)
                    nc.gpsimd.tensor_scalar(mask1[:, q, :], adj_in[:, q, :], 0.0, MASKED, ALU.is_le, ALU.mult)\
                        .then_inc(mask_done, 1)
                if first < 0:
                    pool.wait_ge(st_done, U2 * (n - 1))
                for q in range(QPH):
                    pool.wait_ge(mask_done, QPH * n + q + 1)
                    nc.gpsimd.tensor_copy(mask2[:, n % 2, q, :], mask1[:, q, :]).then_inc(mask2_done, 1)

            nc.gpsimd.memset(sel[SROWS:AROWS, :], 0.0).then_inc(sel_step, 1)
            for s in range(3):
                pool.wait_ge(sel_step, s + 1)
                nc.gpsimd.affine_select(out=sel[SROWS:AROWS, :], in_=sel[SROWS:AROWS, :], compare_op=ALU.not_equal,
                                        fill=1.0, base=-s * H, pattern=[[-1, H]], channel_multiplier=1)\
                    .then_inc(sel_step, 1)
            pool.wait_ge(sel_step, 4)
            make_masks(0, 1)
            make_masks(1, 0)
            with pool.Fori(2, HALVES) as n:
                make_masks(n, -1)

        @block.tensor
        def _(pe):
            def pass1_start(n):
                pe.wait_ge(packs_loaded, 16 * LOADS * (n // 2 + 1))

            def pass1_unit(n, u):
                qt, h = u // H, u % H
                b2 = (n // 2) % 2
                tile = (n % 2) * QPH + qt
                if u >= S1:
                    pe.wait_ge(s1_free, U1 * n + u - S1 + 1)
                slot = u % S1
                for kk in range(2):
                    last = nc.tensor.matmul(s1_ps[:, slot, kk * HALF:(kk + 1) * HALF],
                                            qpack[0:SROWS, b2, h, bass.ds(tile * P, P)],
                                            kpack[0:SROWS, b2, h, kk * HALF:(kk + 1) * HALF], start=True, stop=True)
                last.then_inc(s1_done, 1)

            def negmax_rows(n):
                pe.wait_ge(neg_step, 4 * (n + 1))
                out = s1_ps[SROWS:AROWS, 0, 0:HALF // 2].bitcast(BF16)
                for qt in range(QPH):
                    last = nc.tensor.transpose(out[:, qt * P:(qt + 1) * P],
                                               negmax[:, qt, :, :].rearrange("p s h -> p (s h)"), t.identb[:, :])
                last.then_inc(negT_done, 1)

            def scores(n, step, j):
                u = step * HPG + j
                h, kt = (step // TPB) * HPG + j, step % TPB
                b2, hf = (n // 2) % 2, n % 2
                slot = u % ST_RING
                holder = u - ST_RING if u >= ST_RING else max(v for v in range(U2) if v % ST_RING == slot) - U2
                pe.wait_ge(exp_done, U2 * n + ST_RING + holder + 1)
                out = st_ps[:, slot, :]
                nc.tensor.matmul(out, kpack[0:AROWS, b2, h, kt * P:(kt + 1) * P],
                                 qpack[0:AROWS, b2, h, bass.ds(hf * HALF, HALF)], start=True, stop=False,
                                 skip_group_check=True)
                for qt in range(QPH):
                    last = nc.tensor.matmul(st_ps[:, slot, qt * P:(qt + 1) * P],
                                            mask2[:, hf, qt, kt * P:(kt + 1) * P], t.identb[:, :],
                                            start=False, stop=(qt == QPH - 1), skip_group_check=True)
                last.then_inc(st_done, 1)

            def values(n, step):
                g, kt = step // TPB, step % TPB
                if kt == 0:
                    pe.wait_ge(v_loaded[g], 16 * n + 16)
                    pe.wait_ge(ctx_done, GROUPS * n + g)
                pe.wait_ge(exp_done, U2 * n + ST_RING + step * HPG + HPG)
                for j in range(HPG):
                    u = step * HPG + j
                    last = nc.tensor.matmul(pv_ps[j * VW:(j + 1) * VW, :], vbuf[g][:, kt, j, :],
                                            probs[:, u % P_RING, :], start=(kt == 0), stop=(kt == TPB - 1))
                last.then_inc(pv_done, 1)

            def half(n, with_next):
                pe.wait_ge(mask2_done, QPH * (n + 1))
                pe.wait_ge(neg_placed, n + 1)
                if with_next:
                    pass1_start(n + 1)
                for step in range(STEPS):
                    for j in range(HPG):
                        scores(n, step, j)
                        if with_next and j < S1_PER_STEP and step * S1_PER_STEP + j < U1:
                            pass1_unit(n + 1, step * S1_PER_STEP + j)
                    if step >= 1:
                        values(n, step - 1)
                    if with_next and step == NEG_AT:
                        negmax_rows(n + 1)
                values(n, STEPS - 1)

            pe.sem_inc(pv_done, 1)
            pe.wait_ge(sel_placed, 2)
            pass1_start(0)
            for u in range(U1):
                pass1_unit(0, u)
            negmax_rows(0)
            with pe.Fori(0, HALVES - 1) as n:
                half(n, True)
            half(HALVES - 1, False)

        @block.vector
        def _(dve):
            def half(n):
                b2, hf = (n // 2) % 2, n % 2
                for u in range(U1):
                    qt, h = u // H, u % H
                    slot = u % S1
                    if h == 0:
                        dve.wait_ge(mask_done, QPH * n + qt + 1)
                    dve.wait_ge(s1_done, U1 * n + u + 1)
                    if u >= 2:
                        dve.wait_ge(s1_free, U1 * n + u - 1)
                    t.alone(dve)
                    nc.vector.tensor_tensor_reduce(out=dump[:, u % 2, :], in0=s1_ps[:, slot, :],
                                                   in1=mask1[:, qt, :], scale=1.0, scalar=-3e38,
                                                   op0=ALU.add, op1=ALU.max, accum_out=rowmax[:, qt, h:h + 1])\
                        .then_inc(s1_free, 1)
                dve.wait_ge(s1_free, U1 * n + U1)
                nc.vector.tensor_scalar(negmax[:, :, 0, :], rowmax[:, :, :], -1.0, None, ALU.mult).then_inc(neg_step, 1)
                dve.wait_ge(neg_step, 4 * n + 1)
                nc.vector.scalar_tensor_tensor(out=negmax_rest[:, :, :], in0=rowmax[:, :, :], scalar=-1.0,
                                               in1=negmax[:, :, 0, :], op0=ALU.mult, op1=ALU.subtract)\
                    .then_inc(neg_step, 1)
                dve.wait_ge(neg_step, 4 * n + 2)
                nc.vector.tensor_copy(negmax[:, :, 1, :], negmax_rest[:, :, :]).then_inc(neg_step, 1)
                dve.wait_ge(neg_step, 4 * n + 3)
                nc.vector.tensor_tensor(negmax[:, :, 2, :], negmax_rest[:, :, :], negmax[:, :, 1, :], ALU.subtract)\
                    .then_inc(neg_step, 1)
                dve.wait_ge(negT_done, n + 1)
                src = s1_ps[SROWS:AROWS, 0, 0:HALF // 2].bitcast(BF16)
                nc.vector.tensor_copy(qpack[SROWS:AROWS, b2, :, bass.ds(hf * HALF, HALF)],
                                      src.unsqueeze(1).broadcast_to([MROWS, H, HALF])).then_inc(neg_placed, 1)

            dve.wait_ge(sel_step, 4)
            for b2 in range(2):
                nc.vector.tensor_copy(kpack[SROWS:AROWS, b2, :, :], sel[SROWS:AROWS, :].unsqueeze(2).broadcast_to([MROWS, H, N]))\
                    .then_inc(sel_placed, 1)
            half(0)
            with dve.Fori(1, HALVES) as n:
                half(n)

        @block.scalar
        def _(act):
            def half(n, last_half):
                for step in range(STEPS):
                    for j in range(HPG):
                        u = step * HPG + j
                        act.wait_ge(st_done, U2 * n + u + 1)
                        if j == 0:
                            act.wait_ge(pv_done, STEPS * n + step)
                        slot = u % ST_RING
                        nc.scalar.activation(probs[:, u % P_RING, :], st_ps[:, slot, :], ACT.Exp, scale=SCALE)\
                            .then_inc(exp_done, 1)
                    if step == TPB:
                        copy_out(n, 0, last_half)
                copy_out(n, 1, last_half)

            def copy_out(n, g, last_half):
                act.wait_ge(pv_done, STEPS * n + (g + 1) * TPB + 1)
                act.wait_ge(ctx_stored[g], 16 * n)
                nc.scalar.activation(ctx_sb[:, g, :], pv_ps[:, :], ACT.Copy).then_inc(ctx_done, 1)
                act.wait_ge(ctx_done, GROUPS * n + g + 1)
                act.dma_start(t.ctx_dram[n, g], ctx_sb[:, g, :]).then_inc(ctx_stored[g], 16)
                if not last_half:
                    load_values(n + 1, g)

            def load_values(n, g):
                act.dma_start(vbuf[g][:, :, :, :].rearrange("p t h w -> p t (h w)"),
                              t.v_dram[n // 2].rearrange("(t p) c -> p t c", p=P)[:, :, g * HPG * VW:(g + 1) * HPG * VW])\
                    .then_inc(v_loaded[g], 16)

            act.sem_inc(exp_done, ST_RING)
            for g in range(GROUPS):
                load_values(0, g)
            with act.Fori(0, HALVES - 1) as n:
                half(n, False)
            half(HALVES - 1, True)
            for g in range(GROUPS):
                act.wait_ge(ctx_stored[g], 16 * HALVES)


def combine(nc, t, x, wo, bo, gate_w, gate_b):
    x_v = x.rearrange("b (h q p) d -> (b h) p q d", q=QPH, p=P)
    ctx = ExitStack()
    with ctx:
        sb = lambda name, shape, dt=F32: ctx.enter_context(nc.sbuf_tensor(name, shape, dt))
        ps = lambda name, shape, dt=F32: ctx.enter_context(nc.psum_tensor(name, shape, dt))
        sem = lambda name: ctx.enter_context(nc.semaphore(name))
        two = lambda name: [sem(f"{name}{p}") for p in range(2)]
        pair = lambda name, shape, dt=F32: [sb(f"{name}{p}", shape, dt) for p in range(2)]
        wo_sb, gw_sb = sb("wo_sb", [P, D]), sb("gw_sb", [P, E])
        bo_row, gb_row = sb("bo_row", [P, D]), sb("gb_row", [P, E])
        raw = pair("raw", [P, GROUPS, HALF])
        xres = pair("xres", [P, QPH, D])
        rsum = pair("rsum", [P, QPH * H])
        cn = pair("cn", [P, QPH * H, HD])
        cnT = pair("cnT", [P, HALF])
        x2 = pair("x2", [P, QPH, D])
        stats, meanvar = pair("stats_", [P, QPH, 6]), pair("meanvar_", [P, QPH, 2])
        vareps, std, rstd = pair("vareps_", [P, QPH]), pair("std_", [P, QPH]), pair("rstd_", [P, QPH])
        xn = pair("xn_", [P, QPH, D])
        xnT = pair("xnT_", [P, HALF])
        logits = pair("logits", [P, QPH, E])
        best, best_index = pair("best", [P, QPH, 8]), pair("best_index", [P, QPH, 8], mybir.dt.uint32)
        kept = two("kept")
        a_ps = ps("a_ps", [P, QPH, GROUPS, P])
        b_ps, y_ps, c_ps = ps("b_ps", [P, QPH, P]), ps("y_ps", [P, QPH, D]), ps("c_ps", [P, QPH, P])
        l_ps = ps("l_ps", [P, QPH, E])
        in_loaded, c_loaded = two("in_loaded"), sem("c_loaded")
        xb_done = two("xb_done")
        a_done, rsum_done, cn_done = sem("a_done"), sem("rsum_done"), sem("cn_done")
        b_done, cnT_done, y_done, x2_done = sem("b_done"), sem("cnT_done"), sem("y_done"), sem("x2_done")
        stat_done, aggr_done, vareps_done = sem("stat_done_"), sem("aggr_done_"), sem("vareps_done_")
        std_done, rstd_done, xn_done = sem("std_done_"), sem("rstd_done_"), sem("xn_done_")
        c_done, xnT_done, l_done, logit_done = sem("c_done"), sem("xnT_done_"), sem("l_done"), sem("logit_done")
        top_done, index_done = sem("top_done"), sem("index_done")
        stored = two("stored")
        gate_step = sem("gate_step")
        block = ctx.enter_context(nc.Block())

        def staggered(eng, stages):
            last = len(stages) - 1

            def step(i, p, known):
                for k, stage in enumerate(stages):
                    if not known or 0 <= i - k < HALVES:
                        stage(i - k, (p + k) % 2, i - k if known else 2)
            for i in range(4):
                step(i, i % 2, True)
            with eng.Fori(2, HALVES // 2) as m:
                for p in range(2):
                    step(2 * m + p, p, False)
            for i in range(HALVES, HALVES + last):
                step(i, i % 2, True)

        @block.sync
        def _(sp):
            sp.dma_start(wo_sb[:, :], wo).then_inc(c_loaded, 16)
            sp.dma_start(gw_sb[:, :], gate_w).then_inc(c_loaded, 16)
            sp.dma_start(bo_row[:, :], bo.partition_broadcast(P)).then_inc(c_loaded, 16)
            sp.dma_start(gb_row[:, :], gate_b.partition_broadcast(P)).then_inc(c_loaded, 16)

            def load(n, p, waits):
                if waits:
                    sp.wait_ge(a_done, n - 1)
                    t.alone(sp)
                    sp.wait_ge(x2_done, n - 1)
                sp.dma_start(raw[p][:, :, :], t.ctx_dram[n].rearrange("g p q -> p g q")).then_inc(in_loaded[p], 16)
                sp.dma_start(xres[p][:, :, :], x_v[n]).then_inc(in_loaded[p], 16)

            for n in range(2):
                load(n, n, False)
            with sp.Fori(1, HALVES // 2) as m:
                for p in range(2):
                    load(2 * m + p, p, True)

        @block.gpsimd
        def _(pool):
            pool.wait_ge(c_loaded, 64)

            def add_bias(n, p, early):
                pool.wait_ge(in_loaded[p], 32 * (n // 2) + 32 if early < 2 else 16 * (n - p) + 32)
                for q in range(QPH):
                    nc.gpsimd.tensor_tensor(xres[p][:, q, :], xres[p][:, q, :], bo_row[:, :], ALU.add)\
                        .then_inc(xb_done[p], 1)

            def store(n, p, early):
                pool.wait_ge(x2_done, n + 1)
                pool.wait_ge(xn_done, QPH * n + QPH)
                rows = lambda dram: dram.rearrange("(n q p) d -> n p q d", q=QPH, p=P)[n]
                pool.dma_start(rows(t.x2_dram), x2[p][:, :, :]).then_inc(stored[p], 16)
                pool.dma_start(rows(t.xn2_dram), xn[p][:, :, :]).then_inc(stored[p], 16)

            staggered(pool, (add_bias, store))
            for p in range(2):
                pool.wait_ge(stored[p], 32 * (HALVES // 2))

        @block.tensor
        def _(pe):
            pe.wait_ge(c_loaded, 64)

            def heads(n, p, early):
                pe.wait_ge(in_loaded[p], 16 * (n - p) + 32)
                if early > 0:
                    pe.wait_ge(cn_done, n)
                for q in range(QPH):
                    for g in range(GROUPS):
                        last = nc.tensor.transpose(a_ps[:, q, g, :], raw[p][:, g, q * P:(q + 1) * P], t.ident[:, :])
                last.then_inc(a_done, 1)

            def turn_back(n, p, early):
                pe.wait_ge(cn_done, n + 1)
                if early > 0:
                    pe.wait_ge(cnT_done, n)
                for q in range(QPH):
                    src = cn[p][:, q * H:(q + 1) * H, :].rearrange("p h d -> p (h d)")
                    last = nc.tensor.transpose(b_ps[:, q, :], src, t.ident[:, :])
                last.then_inc(b_done, 1)

            def project(n, p, early):
                pe.wait_ge(cnT_done, n + 1)
                if early > 0:
                    pe.wait_ge(x2_done, n)
                for q in range(QPH):
                    last = nc.tensor.matmul(y_ps[:, q, :], cnT[p][:, q * P:(q + 1) * P], wo_sb[:, :],
                                            start=True, stop=True)
                last.then_inc(y_done, 1)

            def turn_norm(n, p, early):
                pe.wait_ge(xn_done, QPH * n + QPH)
                if early > 0:
                    pe.wait_ge(xnT_done, n)
                for q in range(QPH):
                    last = nc.tensor.transpose(c_ps[:, q, :], xn[p][:, q, :], t.ident[:, :])
                last.then_inc(c_done, 1)

            def route(n, p, early):
                pe.wait_ge(xnT_done, n + 1)
                if early > 0:
                    pe.wait_ge(logit_done, n)
                for q in range(QPH):
                    last = nc.tensor.matmul(l_ps[:, q, :], xnT[p][:, q * P:(q + 1) * P], gw_sb[:, :],
                                            start=True, stop=True)
                last.then_inc(l_done, 1)

            def one(n, p, early):
                turn_back(n, p, early)

            def two_(n, p, early):
                turn_norm(n, p, early)

            staggered(pe, (heads, lambda *a: (turn_back(*a), project(*a)), lambda *a: (turn_norm(*a), route(*a))))

        @block.scalar
        def _(act):
            def copy_heads(n, p, early):
                act.wait_ge(b_done, n + 1)
                if early > 1:
                    act.wait_ge(y_done, n - 1)
                nc.scalar.activation(cnT[p][:, :], b_ps[:, :, :].rearrange("p q d -> p (q d)"), ACT.Copy)\
                    .then_inc(cnT_done, 1)
                act.wait_ge(vareps_done, n + 1)
                nc.scalar.activation(std[p][:, :], vareps[p][:, :], ACT.Sqrt).then_inc(std_done, 1)

            def copy_norm(n, p, early):
                act.wait_ge(c_done, n + 1)
                if early > 1:
                    act.wait_ge(l_done, n - 1)
                nc.scalar.activation(xnT[p][:, :], c_ps[:, :, :].rearrange("p q d -> p (q d)"), ACT.Copy)\
                    .then_inc(xnT_done, 1)

            staggered(act, (lambda *a: None, copy_heads, copy_norm))
            act.wait_ge(gate_step, 1)
            nc.scalar.activation(t.gate[:, :, 1], t.gate_gap[:, :], ACT.Exp).then_inc(gate_step, 1)

        @block.vector
        def _(dve):
            def divide(n, p, early):
                dve.wait_ge(a_done, n + 1)
                a = a_ps[:, :, :, :].rearrange("p q g (j w) -> p (q g j) w", w=VW)
                nc.vector.reciprocal(rsum[p][:, :], a[:, :, HD]).then_inc(rsum_done, 1)
                dve.wait_ge(rsum_done, n + 1)
                if early > 1:
                    dve.wait_ge(b_done, n - 1)
                nc.vector.tensor_tensor(cn[p][:, :, :], a[:, :, 0:HD],
                                        rsum[p][:, :].unsqueeze(2).broadcast_to([P, QPH * H, HD]), ALU.mult)\
                    .then_inc(cn_done, 1)

            def normalise(n, p, early):
                dve.wait_ge(y_done, n + 1)
                dve.wait_ge(xb_done[p], QPH // 2 * (n - p) + QPH)
                if early > 1:
                    dve.wait_ge(stored[p], 16 * (n - p))
                    dve.wait_ge(c_done, n - 1)
                nc.vector.tensor_tensor(x2[p][:, :, :], y_ps[:, :, :], xres[p][:, :, :], ALU.add).then_inc(x2_done, 1)
                dve.wait_ge(x2_done, n + 1)
                for q in range(QPH):
                    nc.vector.bn_stats(stats[p][:, q, :], x2[p][:, q, :]).then_inc(stat_done, 1)
                for q in range(QPH):
                    dve.wait_ge(stat_done, QPH * n + q + 1)
                    t.alone(dve)
                    nc.vector.bn_aggr(meanvar[p][:, q, :], stats[p][:, q, :]).then_inc(aggr_done, 1)
                dve.wait_ge(aggr_done, QPH * n + QPH)
                nc.vector.tensor_scalar(vareps[p][:, :], meanvar[p][:, :, 1], EPS, None, ALU.add)\
                    .then_inc(vareps_done, 1)
                dve.wait_ge(std_done, n + 1)
                nc.vector.reciprocal(rstd[p][:, :], std[p][:, :]).then_inc(rstd_done, 1)
                dve.wait_ge(rstd_done, n + 1)
                for q in range(QPH):
                    nc.vector.tensor_scalar(xn[p][:, q, :], x2[p][:, q, :], meanvar[p][:, q, 0:1],
                                            rstd[p][:, q:q + 1], ALU.subtract, ALU.mult).then_inc(xn_done, 1)

            def choose(n, p, early):
                dve.wait_ge(l_done, n + 1)
                if early > 1:
                    dve.wait_ge(kept[p], n - p)
                nc.vector.tensor_tensor(logits[p][:, :, :], l_ps[:, :, :],
                                        gb_row[:, :].unsqueeze(1).broadcast_to([P, QPH, E]), ALU.add)\
                    .then_inc(logit_done, 1)
                dve.wait_ge(logit_done, n + 1)
                t.alone(dve)
                for q in range(QPH):
                    nc.vector.max(best[p][:, q, :], logits[p][:, q, :]).then_inc(top_done, 1)
                for q in range(QPH):
                    dve.wait_ge(top_done, QPH * n + q + 1)
                    t.alone(dve)
                    nc.vector.max_index(best_index[p][:, q, :], best[p][:, q, :], logits[p][:, q, :])\
                        .then_inc(index_done, 1)
                dve.wait_ge(index_done, QPH * n + QPH)
                nc.vector.tensor_copy(t.top[:, bass.ds(QPH * n, QPH), :], best[p][:, :, 0:2]).then_inc(kept[p], 1)
                nc.vector.tensor_copy(t.top_index[:, bass.ds(QPH * n, QPH), :], best_index[p][:, :, 0:2])\
                    .then_inc(kept[p], 1)

            dve.wait_ge(c_loaded, 64)
            staggered(dve, (divide, normalise, choose))
            for p in range(2):
                dve.wait_ge(kept[p], HALVES)
            nc.vector.tensor_tensor(t.gate_gap[:, :], t.top[:, :, 1], t.top[:, :, 0], ALU.subtract).then_inc(gate_step, 1)
            dve.wait_ge(gate_step, 2)
            nc.vector.tensor_scalar(t.gate_sum[:, :], t.gate[:, :, 1], 1.0, None, ALU.add).then_inc(gate_step, 1)
            dve.wait_ge(gate_step, 3)
            nc.vector.reciprocal(t.gate[:, :, 0], t.gate_sum[:, :]).then_inc(gate_step, 1)
            dve.wait_ge(gate_step, 4)
            nc.vector.tensor_tensor(t.gate[:, :, 1], t.gate[:, :, 1], t.gate[:, :, 0], ALU.mult).then_inc(gate_step, 1)
            dve.wait_ge(gate_step, 5)


def experts(nc, t, w1, w2, w3, out):
    out_v = out.rearrange("b (t p) d -> (b t) p d", p=P)
    rows = lambda dram: dram.rearrange("(t p) d -> t p d", p=P)
    KH = HID // P
    ctx = ExitStack()
    with ctx:
        sb = lambda name, shape, dt=F32: ctx.enter_context(nc.sbuf_tensor(name, shape, dt))
        ps = lambda name, shape, dt=F32: ctx.enter_context(nc.psum_tensor(name, shape, dt))
        sem = lambda name: ctx.enter_context(nc.semaphore(name))
        two = lambda name: [sem(f"{name}{p}") for p in range(2)]
        pair = lambda name, shape, dt=F32: [sb(f"{name}{p}", shape, dt) for p in range(2)]
        w12_sb = sb("w12_sb", [P, E, 2 * HID])
        w3_sb = sb("w3_sb", [P, E, KH, D])
        iota = sb("iota", [P, E])
        xn_in, x2_in = pair("xn_in", [P, D]), pair("x2_in", [P, D])
        disp, disp2 = pair("disp", [P, E]), pair("disp2", [P, E])
        xT = pair("xT", [P, P])
        silu = pair("silu", [P, HID])
        hidden = pair("hidden", [P, HID])
        hT = pair("hT", [P, HID])
        y = pair("y", [P, D])
        h_ps = [ps(f"h_ps{k}", [P, 2 * HID]) for k in range(3)]
        t_ps = [ps(f"t_ps{p}", [P, HID]) for p in range(2)]
        x_ps = ps("x_ps", [P, P])
        y_ps = [ps(f"yy_ps{p}", [P, D]) for p in range(2)]
        w_loaded, iota_done = sem("w_loaded_"), sem("iota_done")
        x_loaded, xT_ps_done, xT_done = two("x_loaded_"), sem("xT_ps_done"), sem("xT_done_")
        disp_step = sem("disp_step")
        h_done, silu_done, hidden_done = sem("h_done"), sem("silu_done"), sem("hidden_done")
        turned, hT_done, y_done, out_done = sem("turned"), sem("hT_done"), sem("y_done_"), sem("out_done")
        stored = two("stored_")
        block = ctx.enter_context(nc.Block())

        @block.sync
        def _(sp):
            sp.dma_start(w12_sb[:, :, 0:HID], w1.rearrange("e d h -> d e h")).then_inc(w_loaded, 16)
            sp.dma_start(w12_sb[:, :, HID:], w2.rearrange("e d h -> d e h")).then_inc(w_loaded, 16)
            for k in range(KH):
                sp.dma_start(w3_sb[:, :, k, :], w3.rearrange("e (k p) d -> k p e d", p=P)[k]).then_inc(w_loaded, 16)

            def load(tile, p, waits):
                if waits:
                    sp.wait_ge(xT_ps_done, tile - 1)
                    t.alone(sp)
                    sp.wait_ge(out_done, tile - 1)
                sp.dma_start(xn_in[p][:, :], rows(t.xn2_dram)[tile]).then_inc(x_loaded[p], 16)
                sp.dma_start(x2_in[p][:, :], rows(t.x2_dram)[tile]).then_inc(x_loaded[p], 16)

            for tile in range(2):
                load(tile, tile, False)
            with sp.Fori(1, TILES // 2) as m:
                for p in range(2):
                    load(2 * m + p, p, True)

        @block.gpsimd
        def _(pool):
            nc.gpsimd.iota(iota[:, :], [[1, E]], base=0, channel_multiplier=0,
                           allow_small_or_imprecise_dtypes=True).then_inc(iota_done, 1)
            with pool.Fori(0, TILES // 2) as m:
                for p in range(2):
                    pool.wait_ge(out_done, 2 * m + p + 1)
                    pool.dma_start(out_v[2 * m + p], y[p][:, :]).then_inc(stored[p], 16)
            for p in range(2):
                pool.wait_ge(stored[p], 16 * (TILES // 2))

        @block.tensor
        def _(pe):
            pe.wait_ge(w_loaded, 16 * (2 + KH))
            with pe.Fori(0, TILES // 2) as m:
                for p in range(2):
                    tile = 2 * m + p
                    pe.wait_ge(x_loaded[p], 32 * m + 32)
                    pe.wait_ge(xT_done, tile)
                    nc.tensor.transpose(x_ps[:, :], xn_in[p][:, :], t.ident[:, :]).then_inc(xT_ps_done, 1)
                    pe.wait_ge(xT_done, tile + 1)

                    def hiddens(e):
                        at = E * p + e
                        if at >= 3:
                            pe.wait_ge(hidden_done, 2 * E * m + at - 2)
                        else:
                            pe.wait_ge(hidden_done, 2 * E * m)
                        nc.tensor.matmul(h_ps[at % 3][:, :], xT[p][:, :], w12_sb[:, e, :], start=True, stop=True)\
                            .then_inc(h_done, 1)

                    def turn(e):
                        pe.wait_ge(hidden_done, 2 * E * m + E * p + e + 1)
                        if p or e >= 2:
                            pe.wait_ge(hT_done, 2 * E * m + E * p + e - 1)
                        for k in range(KH):
                            last = nc.tensor.transpose(t_ps[e % 2][:, k * P:(k + 1) * P],
                                                       hidden[e % 2][:, k * P:(k + 1) * P], t.ident[:, :])
                        last.then_inc(turned, 1)

                    def down(e):
                        pe.wait_ge(hT_done, 2 * E * m + E * p + e + 1)
                        if e == 0:
                            pe.wait_ge(out_done, tile - p)
                        for k in range(KH):
                            last = nc.tensor.matmul(y_ps[p][:, :], hT[e % 2][:, k * P:(k + 1) * P], w3_sb[:, e, k, :],
                                                    start=(e == 0 and k == 0), stop=(e == E - 1 and k == KH - 1))
                        last.then_inc(y_done, 1)

                    for e in range(E + 2):
                        if e < E:
                            hiddens(e)
                        if 1 <= e <= E:
                            turn(e - 1)
                        if e >= 2:
                            down(e - 2)

        @block.scalar
        def _(act):
            with act.Fori(0, TILES // 2) as m:
                for p in range(2):
                    act.wait_ge(xT_ps_done, 2 * m + p + 1)
                    nc.scalar.activation(xT[p][:, :], x_ps[:, :], ACT.Copy).then_inc(xT_done, 1)
                    for e in range(E + 1):
                        if e < E:
                            act.wait_ge(h_done, 2 * E * m + E * p + e + 1)
                            if p or e >= 2:
                                act.wait_ge(hidden_done, 2 * E * m + E * p + e - 1)
                            nc.scalar.activation(silu[e % 2][:, :], h_ps[(E * p + e) % 3][:, 0:HID], ACT.Silu)\
                                .then_inc(silu_done, 1)
                        if e >= 1:
                            act.wait_ge(turned, 2 * E * m + E * p + e)
                            if p or e >= 3:
                                act.wait_ge(y_done, 2 * E * m + E * p + e - 2)
                            nc.scalar.activation(hT[(e - 1) % 2][:, :], t_ps[(e - 1) % 2][:, :], ACT.Copy)\
                                .then_inc(hT_done, 1)

        @block.vector
        def _(dve):
            dve.wait_ge(iota_done, 1)
            with dve.Fori(0, TILES // 2) as m:
                for p in range(2):
                    tile = 2 * m + p
                    nc.vector.tensor_scalar(disp2[p][:, :], iota[:, :], t.top_index[:, tile, 1:2], t.gate[:, tile, 1:2],
                                            ALU.is_equal, ALU.mult).then_inc(disp_step, 1)
                    nc.vector.tensor_scalar(disp[p][:, :], iota[:, :], t.top_index[:, tile, 0:1], t.gate[:, tile, 0:1],
                                            ALU.is_equal, ALU.mult).then_inc(disp_step, 1)
                    dve.wait_ge(disp_step, 3 * tile + 2)
                    nc.vector.tensor_tensor(disp[p][:, :], disp[p][:, :], disp2[p][:, :], ALU.add).then_inc(disp_step, 1)
                    dve.wait_ge(disp_step, 3 * tile + 3)
                    for e in range(E):
                        dve.wait_ge(silu_done, 2 * E * m + E * p + e + 1)
                        if p or e >= 2:
                            dve.wait_ge(turned, 2 * E * m + E * p + e - 1)
                        nc.vector.scalar_tensor_tensor(out=hidden[e % 2][:, :],
                                                       in0=h_ps[(E * p + e) % 3][:, HID:], scalar=disp[p][:, e:e + 1],
                                                       in1=silu[e % 2][:, :], op0=ALU.mult, op1=ALU.mult)\
                            .then_inc(hidden_done, 1)
                    dve.wait_ge(y_done, 2 * E * m + E * p + E)
                    dve.wait_ge(x_loaded[p], 32 * m + 32)
                    dve.wait_ge(stored[p], 16 * m)
                    nc.vector.tensor_tensor(y[p][:, :], y_ps[p][:, :], x2_in[p][:, :], ALU.add).then_inc(out_done, 1)


class Shared:

    CONSTS = 3

    def alone(self, eng):
        eng.sem_inc(self.waits_carried, 1)


def program(nc, x, adj, wq, wk, wv, wo, bo, gate_w, gate_b, w1, w2, w3, out):
    t = Shared()
    ctx = ExitStack()
    with ctx:
        sb = lambda name, shape, dt=F32: ctx.enter_context(nc.sbuf_tensor(name, shape, dt))
        t.ident, t.identb = sb("ident", [P, P]), sb("identb", [P, P], BF16)
        t.top, t.top_index = sb("top", [P, TILES, 2]), sb("top_index", [P, TILES, 2])
        t.gate, t.gate_gap, t.gate_sum = sb("gate", [P, TILES, 2]), sb("gate_gap", [P, TILES]), sb("gate_sum", [P, TILES])
        t.consts_done = ctx.enter_context(nc.semaphore("consts_done"))
        t.waits_carried = ctx.enter_context(nc.semaphore("waits_carried"))
        t.parts_dram = nc.dram_tensor("parts_dram", (B, 2, 3, P, N), BF16, kind="Internal").ap()
        t.v_dram = nc.dram_tensor("v_dram", (B, N, H * VW), F32, kind="Internal").ap()
        t.ctx_dram = nc.dram_tensor("ctx_dram", (HALVES, GROUPS, P, HALF), F32, kind="Internal").ap()
        t.x2_dram = nc.dram_tensor("x2_dram", (TOKENS, D), F32, kind="Internal").ap()
        t.xn2_dram = nc.dram_tensor("xn2_dram", (TOKENS, D), F32, kind="Internal").ap()
        with nc.Block() as block:
            @block.gpsimd
            def _(pool):
                nc.gpsimd.memset(t.ident[:, :], 0.0).then_inc(t.consts_done, 1)
                pool.wait_ge(t.consts_done, 1)
                nc.gpsimd.affine_select(out=t.ident[:, :], in_=t.ident[:, :], compare_op=ALU.not_equal, fill=1.0,
                                        base=0, pattern=[[-1, P]], channel_multiplier=1).then_inc(t.consts_done, 1)
                pool.wait_ge(t.consts_done, 2)
                nc.gpsimd.tensor_copy(t.identb[:, :], t.ident[:, :]).then_inc(t.consts_done, 1)
        prepare(nc, t, x, wq, wk, wv)
        attention(nc, t, adj)
        combine(nc, t, x, wo, bo, gate_w, gate_b)
        experts(nc, t, w1, w2, w3, out)


_INS = ["x", "adj", "L0_gnn_Wq", "L0_gnn_Wk", "L0_gnn_Wv", "L0_gnn_Wo", "L0_gnn_bo", "L0_ffn_gate_w", "L0_ffn_gate_b",
        "L0_ffn_w1", "L0_ffn_w2", "L0_ffn_w3"]
_OUTS = [((B, N, D), "float32")]


def kernel(**inputs):
    import numpy as _np
    import concourse.bacc as _bacc
    from concourse import mybir as _mybir
    from concourse.bass_utils import run_bass_kernel_spmd as _run

    nc = _bacc.Bacc("TRN2", target_bir_lowering=False, num_devices=1)
    nc.disable_value_cache = True
    arrays, args = {}, []
    for name in _INS:
        a = _np.ascontiguousarray(inputs[name])
        arrays[f"in_{name}_dram"] = a
        args.append(nc.dram_tensor(f"in_{name}_dram", a.shape, _mybir.dt.from_np(a.dtype), kind="ExternalInput").ap())
    for i, (shape, dtype) in enumerate(_OUTS):
        dt = _mybir.dt.from_np(_np.dtype(dtype))
        args.append(nc.dram_tensor(f"out_{i}_dram", shape, dt, kind="ExternalOutput").ap())
    program(nc, *args)
    r = _run(nc, [arrays], core_ids=[0])
    got = tuple(r.results[0][f"out_{i}_dram"] for i in range(len(_OUTS)))
    return got[0]
```

```python
from contextlib import ExitStack

import concourse.bass as bass
from concourse import mybir

F32 = mybir.dt.float32
BF16 = mybir.dt.bfloat16
I32 = mybir.dt.int32
ALU = mybir.AluOpType
ACT = mybir.ActivationFunctionType

P = 128
B, N, D = 8, 1024, 128
H, HD = 8, 16
TOKENS = B * N
TILES = TOKENS // P
TPB = N // P
E, HID = 16, 256
EPS = 1e-5
SCALE = HD ** -0.5

Q_BLOCKS = (0, 0, 1, 1, 0, 2)
K_BLOCKS = (0, 1, 0, 1, 2, 0)
SROWS = HD * len(Q_BLOCKS)
MROWS = 3 * H
AROWS = SROWS + MROWS
HALF = 512
HALVES = TOKENS // HALF
QPH = HALF // P
HPG = 4
GROUPS = H // HPG
VW = 32
ZEROS = 512
SPLIT = 5
MASKED = -2.0 ** 100


def stage_semaphores(nc, ctx, tag=""):
    numbers = []

    def sem(name):
        handle = ctx.enter_context(nc.semaphore(name + tag))
        numbers.append(handle.num)
        return handle

    def clear():
        with nc.Block() as block:
            @block.gpsimd
            def _(pool):
                for a in numbers:
                    if a - 1 not in numbers:
                        b = a
                        while b in numbers:
                            b += 1
                        pool.sem_clear(range(a, b))

    ctx.callback(clear)
    return sem


def prepare(nc, t, x, wq, wk, wv):
    x_v = x.rearrange("b (t p) d -> b p t d", p=P)
    ctx = ExitStack()
    with ctx:
        sb = lambda name, shape, dt=F32: ctx.enter_context(nc.sbuf_tensor(name, shape, dt))
        sem = stage_semaphores(nc, ctx)
        two = lambda name: [sem(f"{name}{p}") for p in range(2)]
        w_in = [sb(f"w_in{k}", [P, D]) for k in range(3)]
        xn = [sb(f"xn{p}", [P, TPB, D]) for p in range(2)]
        xnT = [sb(f"xnT{p}", [P, N]) for p in range(2)]
        stats = [sb(f"stats{p}", [P, TPB, 6]) for p in range(2)]
        meanvar = [sb(f"meanvar{p}", [P, TPB, 2]) for p in range(2)]
        vareps = [sb(f"vareps{p}", [P, TPB]) for p in range(2)]
        std = [sb(f"std{p}", [P, TPB]) for p in range(2)]
        rstd = [sb(f"rstd{p}", [P, TPB]) for p in range(2)]
        qk32 = [sb(f"qk32{p}", [P, 2, N]) for p in range(2)]
        rest = [sb(f"rest{p}", [P, 2, N]) for p in range(2)]
        parts = [sb(f"parts{p}", [P, 2, 3, N], BF16) for p in range(2)]
        vpad = [sb(f"vpad{p}", [P, TPB, H, VW]) for p in range(2)]
        xT_ps = [ctx.enter_context(nc.psum_tensor(f"xT_ps{p}", [P, N], F32)) for p in range(2)]
        out_ps = ctx.enter_context(nc.psum_tensor("out_ps", [P, 4, HALF], F32))
        w_loaded, x_loaded = sem("w_loaded"), two("x_loaded")
        stat_done, aggr_done, vareps_done = two("stat_done"), two("aggr_done"), two("vareps_done")
        std_done, rstd_done, xn_done = two("std_done"), two("rstd_done"), two("xn_done")
        xT_done, xnT_done = two("xT_done"), two("xnT_done")
        chunk_done, chunk_free = sem("chunk_done"), sem("chunk_free")
        hi_done, rest_done, mid_done, lo_done = two("hi_done"), two("rest_done"), two("mid_done"), two("lo_done")
        parts_stored, v_stored, pad_done = two("parts_stored"), two("v_stored"), sem("pad_done")
        CH = 6
        block = ctx.enter_context(nc.Block())

        @block.sync
        def _(sp):
            for k, w in enumerate((wq, wk, wv)):
                sp.dma_start(w_in[k][:, :], w).then_inc(w_loaded, 16)

            def load(i, first=False):
                for p in range(2):
                    if not first:
                        sp.wait_ge(x_loaded[p], 16 * i)
                    sp.dma_start(t.x2[:, bass.ds((2 * i + p) * TPB, TPB), :], x_v[2 * i + p]).then_inc(x_loaded[p], 16)

            def store(i):
                for p in range(2):
                    sp.wait_ge(chunk_free, 2 * CH * i + CH * (p + 1))
                    sp.dma_start(t.v_dram[2 * i + p].rearrange("(t p) c -> p t c", p=P),
                                 vpad[p][:, :, :, :].rearrange("p t h w -> p t (h w)")).then_inc(v_stored[p], 16)
                    sp.wait_ge(lo_done[p], 2 * i + 2)
                    sp.dma_start(t.parts_dram[2 * i + p].rearrange("w s p n -> p w s n"), parts[p][:, :, :, :])\
                        .then_inc(parts_stored[p], 16)

            load(0, first=True)
            load(1)
            with sp.Fori(0, B // 2 - 2) as i:
                load(i + 2)
                store(i)
            with sp.Fori(B // 2 - 2, B // 2) as i:
                store(i)
            for p in range(2):
                sp.wait_ge(v_stored[p], 16 * (B // 2))
                sp.wait_ge(parts_stored[p], 16 * (B // 2))

        @block.vector
        def _(dve):
            for p in range(2):
                dve.memset(vpad[p][:, :, :, HD:HD + 1], 1.0).then_inc(pad_done, 1)
                dve.memset(vpad[p][:, :, :, HD + 1:VW], 0.0).then_inc(pad_done, 1)

            def statistics(i):
                for p in range(2):
                    dve.wait_ge(x_loaded[p], 16 * i + 16)
                    for t_ in range(TPB):
                        nc.vector.bn_stats(stats[p][:, t_, :], t.x2[:, (2 * i + p) * TPB + t_, :]).then_inc(stat_done[p], 1)
                    dve.wait_ge(stat_done[p], TPB * i + TPB)
                    t.alone(dve)
                    for t_ in range(TPB):
                        nc.vector.bn_aggr(meanvar[p][:, t_, :], stats[p][:, t_, :]).then_inc(aggr_done[p], 1)
                    dve.wait_ge(aggr_done[p], TPB * i + TPB)
                    nc.vector.tensor_scalar(vareps[p][:, :], meanvar[p][:, :, 1], EPS, None, ALU.add)\
                        .then_inc(vareps_done[p], 1)

            def normalise(i, first=False):
                for p in range(2):
                    dve.wait_ge(std_done[p], i + 1)
                    nc.vector.reciprocal(rstd[p][:, :], std[p][:, :]).then_inc(rstd_done[p], 1)
                    dve.wait_ge(rstd_done[p], i + 1)
                    if not first:
                        dve.wait_ge(xT_done[p], i)
                    for t_ in range(TPB):
                        nc.vector.tensor_scalar(xn[p][:, t_, :], t.x2[:, (2 * i + p) * TPB + t_, :], meanvar[p][:, t_, 0:1],
                                                rstd[p][:, t_:t_ + 1], ALU.subtract, ALU.mult)\
                            .then_inc(xn_done[p], 1)

            def split(i, first=False):
                for p in range(2):
                    for k in range(2):
                        dve.wait_ge(hi_done[p], 2 * i + k + 1)
                        if not first:
                            dve.wait_ge(lo_done[p], 2 * i)
                        nc.vector.tensor_tensor(rest[p][:, k, :], qk32[p][:, k, :], parts[p][:, k, 0, :],
                                                ALU.subtract).then_inc(rest_done[p], 1)
                    for k in range(2):
                        dve.wait_ge(rest_done[p], 2 * i + k + 1)
                        nc.vector.tensor_copy(parts[p][:, k, 1, :], rest[p][:, k, :]).then_inc(mid_done[p], 1)

            statistics(0)
            normalise(0, first=True)
            statistics(1)
            normalise(1)
            statistics(2)
            split(0, first=True)
            with dve.Fori(2, B // 2 - 1) as i:
                normalise(i)
                statistics(i + 1)
                split(i - 1)
            normalise(B // 2 - 1)
            split(B // 2 - 2)
            split(B // 2 - 1)

        @block.tensor
        def _(pe):
            pe.wait_ge(w_loaded, 48)
            pe.wait_ge(t.consts_done, t.CONSTS)

            def pair(i, first=False):
                for p in range(2):
                    if not first:
                        pe.wait_ge(xnT_done[p], i)
                    for t_ in range(TPB):
                        pe.wait_ge(xn_done[p], TPB * i + t_ + 1)
                        last = nc.tensor.transpose(xT_ps[p][:, t_ * P:(t_ + 1) * P], xn[p][:, t_, :], t.ident[:, :])
                    last.then_inc(xT_done[p], 1)
                for p in range(2):
                    pe.wait_ge(xnT_done[p], i + 1)
                    for c in range(CH):
                        at = CH * p + c
                        if at >= 4:
                            pe.wait_ge(chunk_free, 2 * CH * i + at - 3)
                        elif not first:
                            pe.wait_ge(chunk_free, 2 * CH * i)
                        bank, half = out_ps[:, at % 4, :], c % 2
                        if c < 4:
                            last = nc.tensor.matmul(bank, w_in[c // 2][:, :], xnT[p][:, half * HALF:(half + 1) * HALF],
                                                    start=True, stop=True)
                        else:
                            for j in range(QPH):
                                tok = (half * QPH + j) * P
                                last = nc.tensor.matmul(bank[:, j * P:(j + 1) * P], xnT[p][:, tok:tok + P], w_in[2][:, :],
                                                        start=True, stop=True)
                        last.then_inc(chunk_done, 1)

            pair(0, first=True)
            with pe.Fori(1, B // 2) as i:
                pair(i)

        @block.scalar
        def _(act):
            act.wait_ge(pad_done, 4)

            def deviations(i):
                for p in range(2):
                    act.wait_ge(vareps_done[p], i + 1)
                    nc.scalar.activation(std[p][:, :], vareps[p][:, :], ACT.Sqrt).then_inc(std_done[p], 1)

            def pair(i, first=False, last=False):
                for p in range(2):
                    act.wait_ge(xT_done[p], i + 1)
                    if not first:
                        act.wait_ge(chunk_done, 2 * CH * i)
                    nc.scalar.activation(xnT[p][:, :], xT_ps[p][:, :], ACT.Copy).then_inc(xnT_done[p], 1)
                for p in range(2):
                    if not first:
                        act.wait_ge(rest_done[p], 2 * i)
                        act.wait_ge(v_stored[p], 16 * i)
                    for c in range(CH):
                        act.wait_ge(chunk_done, 2 * CH * i + CH * p + c + 1)
                        bank, half = out_ps[:, (CH * p + c) % 4, :], c % 2
                        if c < 4:
                            nc.scalar.activation(qk32[p][:, c // 2, half * HALF:(half + 1) * HALF], bank, ACT.Copy)\
                                .then_inc(chunk_free, 1)
                        else:
                            src = bank.rearrange("p (t h d) -> p t h d", h=H, d=HD)
                            nc.scalar.activation(vpad[p][:, half * QPH:(half + 1) * QPH, :, 0:HD], src, ACT.Copy)\
                                .then_inc(chunk_free, 1)
                    if not first:
                        act.wait_ge(parts_stored[p], 16 * i)
                    act.wait_ge(chunk_free, 2 * CH * i + CH * (p + 1))
                    for k in range(2):
                        nc.scalar.activation(parts[p][:, k, 0, :], qk32[p][:, k, :], ACT.Copy).then_inc(hi_done[p], 1)
                    if p == 0 and not last:
                        deviations(i + 1)

            deviations(0)
            pair(0, first=True)
            with act.Fori(1, B // 2 - 1) as i:
                pair(i)
            pair(B // 2 - 1, last=True)

        @block.gpsimd
        def _(pool):
            with pool.Fori(0, B // 2) as i:
                for p in range(2):
                    for k in range(2):
                        pool.wait_ge(mid_done[p], 2 * i + k + 1)
                        nc.gpsimd.tensor_tensor(parts[p][:, k, 2, :], rest[p][:, k, :], parts[p][:, k, 1, :],
                                                ALU.subtract).then_inc(lo_done[p], 1)


def attention(nc, t, adj, grp, scatter, fill=()):
    adj_v = adj.rearrange("b (t p) k -> b t p k", p=P)
    g0, graphs = grp.graph0, grp.graphs
    halves = 2 * graphs
    ctx = ExitStack()
    with ctx:
        sb = lambda name, shape, dt=F32: ctx.enter_context(nc.sbuf_tensor(name + grp.tag, shape, dt))
        ps = lambda name, shape, dt=F32: ctx.enter_context(nc.psum_tensor(name + grp.tag, shape, dt))
        sem = stage_semaphores(nc, ctx, grp.tag)
        ADJ_RING, ST_RING, P_RING, S1 = 4, 3, 8, 2
        qpack = sb("qpack", [P, 2, H, N], BF16)
        kpack = sb("kpack", [P, 2, H, N], BF16)
        mask1 = sb("mask1", [P, QPH, N], BF16)
        mask2 = sb("mask2", [P, 2, QPH, N], BF16)
        adj_in = sb("adj_in", [P, ADJ_RING, N], I32)
        vbuf = [sb(f"vbuf{g}", [P, TPB, HPG, VW]) for g in range(GROUPS)]
        probs = sb("probs", [P, P_RING, HALF])
        dump = sb("dump", [P, 2, N], BF16)
        rowmax = sb("rowmax", [P, QPH, H])
        negmax_rest = sb("negmax_rest", [P, QPH, H])
        negmax = sb("negmax", [P, QPH, 3, H], BF16)
        ctx_sb = sb("ctx_sb", [P, GROUPS, HALF])
        s1_ps = ps("s1_ps", [P, S1, N])
        st_ps = ps("st_ps", [P, ST_RING, HALF])
        pv_ps = ps("pv_ps", [P, HALF])
        sel = sb("sel", [P, H], BF16)
        sel_step, sel_placed = sem("sel_step"), sem("sel_placed")
        packs_loaded = sem("packs_loaded")
        adj_loaded = [sem(f"adj_loaded{r}") for r in range(ADJ_RING)]
        v_loaded = [sem(f"v_loaded{g}") for g in range(GROUPS)]
        mask_done, mask2_done, s1_done, s1_free = sem("mask_done"), sem("mask2_done"), sem("s1_done"), sem("s1_free")
        neg_step, negT_done, neg_placed = sem("neg_step"), sem("negT_done"), sem("neg_placed")
        st_done, exp_done, pv_done, ctx_done = sem("st_done"), sem("exp_done"), sem("pv_done"), sem("ctx_done")
        ctx_stored = [sem(f"ctx_stored{g}") for g in range(GROUPS)]
        U1 = QPH * H
        STEPS = GROUPS * TPB
        U2 = STEPS * HPG
        S1_NUM, S1_DEN = 5, 8
        NEG_AT = -(-U1 * S1_DEN // S1_NUM // HPG) + 1
        LOADS = 2 * len(Q_BLOCKS)
        assert halves % 4 == 2
        block = ctx.enter_context(nc.Block())

        @block.sync
        def _(sp):
            def load_graph(b, early):
                if early > 0:
                    sp.wait_ge(packs_loaded, 16 * LOADS * b)
                if early > 1:
                    t.alone(sp)
                    sp.wait_ge(st_done, 2 * U2 * (b - 1))
                for pack, w, blocks in ((qpack, 0, Q_BLOCKS), (kpack, 1, K_BLOCKS)):
                    for j, part in enumerate(blocks):
                        sp.dma_start(pack[j * HD:(j + 1) * HD, b % 2, :, :],
                                     t.parts_dram[g0 + b, w, part].rearrange("(h d) n -> d h n", d=HD))\
                            .then_inc(packs_loaded, 16)
                for qt in range(TPB):
                    if early > 0 or qt >= ADJ_RING:
                        sp.wait_ge(mask_done, TPB * b + qt - ADJ_RING + 1)
                    sp.dma_start(adj_in[:, qt % ADJ_RING, :], adj_v[g0 + b, qt]).then_inc(adj_loaded[qt % ADJ_RING], 16)

            load_graph(0, 0)
            load_graph(1, 1)
            for other in fill:
                sp.dma_start(other.xs_dram.rearrange("(p a z) d -> p a (z d)", p=P, z=ZEROS // D),
                             t.zeros[:, :].unsqueeze(1).broadcast_to([P, other.slot_tiles * D // ZEROS, ZEROS]))\
                    .then_inc(t.zeroed, 16)
            with sp.Fori(2, graphs) as b:
                load_graph(b, 2)

        @block.gpsimd
        def _(pool):
            def make_masks(n, first):
                for q in range(QPH):
                    pool.wait_ge(adj_loaded[q], 16 * n + 16)
                    if first < 1:
                        pool.wait_ge(mask2_done, QPH * (n - 1) + q + 1)
                        pool.wait_ge(s1_free, U1 * (n - 1) + H * (q + 1))
                    t.alone(pool)
                    nc.gpsimd.tensor_scalar(mask1[:, q, :], adj_in[:, q, :], 0.0, MASKED, ALU.is_le, ALU.mult)\
                        .then_inc(mask_done, 1)
                if first < 0:
                    pool.wait_ge(st_done, U2 * (n - 1))
                for q in range(QPH):
                    pool.wait_ge(mask_done, QPH * n + q + 1)
                    nc.gpsimd.tensor_copy(mask2[:, n % 2, q, :], mask1[:, q, :]).then_inc(mask2_done, 1)

            nc.gpsimd.memset(sel[SROWS:AROWS, :], 0.0).then_inc(sel_step, 1)
            for s in range(3):
                pool.wait_ge(sel_step, s + 1)
                nc.gpsimd.affine_select(out=sel[SROWS:AROWS, :], in_=sel[SROWS:AROWS, :], compare_op=ALU.not_equal,
                                        fill=1.0, base=-s * H, pattern=[[-1, H]], channel_multiplier=1)\
                    .then_inc(sel_step, 1)
            pool.wait_ge(sel_step, 4)
            make_masks(0, 1)
            make_masks(1, 0)
            half = (len(scatter.rows) + 1) // 2 if scatter else 0
            if scatter:
                scatter.run(pool, 0, half)
            make_masks(2, -1)
            if scatter:
                scatter.run(pool, half, len(scatter.rows))
            with pool.Fori(3, halves) as n:
                make_masks(n, -1)
            if scatter:
                scatter.wait(pool)

        @block.tensor
        def _(pe):
            def pass1_start(graph):
                pe.wait_ge(packs_loaded, 16 * LOADS * (graph + 1))

            def pass1_unit(n, r, u):
                qt, h = u // H, u % H
                b2 = (r // 2) % 2
                tile = (r % 2) * QPH + qt
                if u >= S1:
                    pe.wait_ge(s1_free, U1 * n + u - S1 + 1)
                slot = u % S1
                for kk in range(2):
                    last = nc.tensor.matmul(s1_ps[:, slot, kk * HALF:(kk + 1) * HALF],
                                            qpack[0:SROWS, b2, h, tile * P:(tile + 1) * P],
                                            kpack[0:SROWS, b2, h, kk * HALF:(kk + 1) * HALF], start=True, stop=True)
                last.then_inc(s1_done, 1)

            def negmax_rows(n):
                pe.wait_ge(neg_step, 4 * (n + 1))
                out = s1_ps[SROWS:AROWS, 0, 0:HALF // 2].bitcast(BF16)
                for qt in range(QPH):
                    last = nc.tensor.transpose(out[:, qt * P:(qt + 1) * P],
                                               negmax[:, qt, :, :].rearrange("p s h -> p (s h)"), t.identb[:, :])
                last.then_inc(negT_done, 1)

            def scores(n, r, step, j):
                u = step * HPG + j
                h, kt = (step // TPB) * HPG + j, step % TPB
                b2, hf = (r // 2) % 2, r % 2
                slot = u % ST_RING
                holder = u - ST_RING if u >= ST_RING else max(v for v in range(U2) if v % ST_RING == slot) - U2
                pe.wait_ge(exp_done, U2 * n + ST_RING + holder + 1)
                out = st_ps[:, slot, :]
                nc.tensor.matmul(out, kpack[0:AROWS, b2, h, kt * P:(kt + 1) * P],
                                 qpack[0:AROWS, b2, h, hf * HALF:(hf + 1) * HALF], start=True, stop=False,
                                 skip_group_check=True)
                for qt in range(QPH):
                    last = nc.tensor.matmul(st_ps[:, slot, qt * P:(qt + 1) * P],
                                            mask2[:, hf, qt, kt * P:(kt + 1) * P], t.identb[:, :],
                                            start=False, stop=(qt == QPH - 1), skip_group_check=True)
                last.then_inc(st_done, 1)

            def values(n, first, step):
                g, kt = step // TPB, step % TPB
                if kt == 0:
                    pe.wait_ge(v_loaded[g], 16 * n + 16)
                    if first < 1 or g > 0:
                        pe.wait_ge(ctx_done, GROUPS * n + g)
                pe.wait_ge(exp_done, U2 * n + ST_RING + step * HPG + HPG)
                for j in range(HPG):
                    u = step * HPG + j
                    last = nc.tensor.matmul(pv_ps[j * VW:(j + 1) * VW, :], vbuf[g][:, kt, j, :],
                                            probs[:, u % P_RING, :], start=(kt == 0), stop=(kt == TPB - 1))
                last.then_inc(pv_done, 1)

            def half(n, r, graph, first, with_next):
                pe.wait_ge(mask2_done, QPH * (n + 1))
                pe.wait_ge(neg_placed, n + 1)
                if with_next and r % 2 == 1:
                    pass1_start(graph + 1)
                for step in range(STEPS):
                    for j in range(HPG):
                        scores(n, r, step, j)
                        at = step * HPG + j
                        if with_next:
                            for u in range(*(min(U1, k * S1_NUM // S1_DEN) for k in (at, at + 1))):
                                pass1_unit(n + 1, r + 1, u)
                    if step >= 1:
                        values(n, first, step - 1)
                    if with_next and step == NEG_AT:
                        negmax_rows(n + 1)
                values(n, first, STEPS - 1)

            pe.sem_inc(pv_done, 1)
            pass1_start(0)
            for u in range(U1):
                pass1_unit(0, 0, u)
            pe.wait_ge(sel_placed, 2)
            negmax_rows(0)
            half(0, 0, 0, 1, True)
            with pe.Fori(0, (halves - 2) // 4) as m:
                for r in range(1, 5):
                    half(4 * m + r, r, 2 * m + r // 2, 0, True)
            half(halves - 1, (halves - 1) % 4, graphs - 1, 0, False)

        @block.vector
        def _(dve):
            def half(n):
                b2, hf = (n // 2) % 2, n % 2
                for u in range(U1):
                    qt, h = u // H, u % H
                    slot = u % S1
                    if h == 0:
                        dve.wait_ge(mask_done, QPH * n + qt + 1)
                    dve.wait_ge(s1_done, U1 * n + u + 1)
                    if u >= 2:
                        dve.wait_ge(s1_free, U1 * n + u - 1)
                    t.alone(dve)
                    nc.vector.tensor_tensor_reduce(out=dump[:, u % 2, :], in0=s1_ps[:, slot, :],
                                                   in1=mask1[:, qt, :], scale=1.0, scalar=-3e38,
                                                   op0=ALU.add, op1=ALU.max, accum_out=rowmax[:, qt, h:h + 1])\
                        .then_inc(s1_free, 1)
                dve.wait_ge(s1_free, U1 * n + U1)
                nc.vector.tensor_scalar(negmax[:, :, 0, :], rowmax[:, :, :], -1.0, None, ALU.mult).then_inc(neg_step, 1)
                dve.wait_ge(neg_step, 4 * n + 1)
                nc.vector.scalar_tensor_tensor(out=negmax_rest[:, :, :], in0=rowmax[:, :, :], scalar=-1.0,
                                               in1=negmax[:, :, 0, :], op0=ALU.mult, op1=ALU.subtract)\
                    .then_inc(neg_step, 1)
                dve.wait_ge(neg_step, 4 * n + 2)
                nc.vector.tensor_copy(negmax[:, :, 1, :], negmax_rest[:, :, :]).then_inc(neg_step, 1)
                dve.wait_ge(neg_step, 4 * n + 3)
                nc.vector.tensor_tensor(negmax[:, :, 2, :], negmax_rest[:, :, :], negmax[:, :, 1, :], ALU.subtract)\
                    .then_inc(neg_step, 1)
                dve.wait_ge(negT_done, n + 1)
                src = s1_ps[SROWS:AROWS, 0, 0:HALF // 2].bitcast(BF16)
                nc.vector.tensor_copy(qpack[SROWS:AROWS, b2, :, bass.ds(hf * HALF, HALF)],
                                      src.unsqueeze(1).broadcast_to([MROWS, H, HALF])).then_inc(neg_placed, 1)

            half(0)
            with dve.Fori(1, halves) as n:
                half(n)

        @block.scalar
        def _(act):
            def half(n, first, last_half):
                for step in range(STEPS):
                    for j in range(HPG):
                        u = step * HPG + j
                        act.wait_ge(st_done, U2 * n + u + 1)
                        if j == 0 and not (first and step == 0):
                            act.wait_ge(pv_done, STEPS * n + step)
                        slot = u % ST_RING
                        nc.scalar.activation(probs[:, u % P_RING, :], st_ps[:, slot, :], ACT.Exp, scale=SCALE)\
                            .then_inc(exp_done, 1)
                    if step == TPB:
                        copy_out(n, 0, first, last_half)
                copy_out(n, 1, first, last_half)

            def copy_out(n, g, first, last_half):
                act.wait_ge(pv_done, STEPS * n + (g + 1) * TPB + 1)
                if not first:
                    act.wait_ge(ctx_stored[g], 16 * n)
                nc.scalar.activation(ctx_sb[:, g, :], pv_ps[:, :], ACT.Copy).then_inc(ctx_done, 1)
                act.wait_ge(ctx_done, GROUPS * n + g + 1)
                act.dma_start(t.ctx_dram[2 * g0 + n, g], ctx_sb[:, g, :]).then_inc(ctx_stored[g], 16)
                if not last_half:
                    load_values(n + 1, g)

            def load_values(n, g):
                act.dma_start(vbuf[g][:, :, :, :].rearrange("p t h w -> p t (h w)"),
                              t.v_dram[g0 + n // 2].rearrange("(t p) c -> p t c", p=P)[:, :, g * HPG * VW:(g + 1) * HPG * VW])\
                    .then_inc(v_loaded[g], 16)

            act.sem_inc(exp_done, ST_RING)
            for g in range(GROUPS):
                load_values(0, g)
            act.wait_ge(sel_step, 4)
            for b2 in range(2):
                nc.scalar.activation(kpack[SROWS:AROWS, b2, :, :], sel[SROWS:AROWS, :].unsqueeze(2).broadcast_to([MROWS, H, N]),
                                     ACT.Copy).then_inc(sel_placed, 1)
            half(0, True, False)
            with act.Fori(1, halves - 1) as n:
                half(n, False, False)
            half(halves - 1, False, True)
            for g in range(GROUPS):
                act.wait_ge(ctx_stored[g], 16 * halves)


def staggered(eng, count, stages, unroll=2, before=None):
    depth = max(lag for lag, _ in stages) + 1
    peeled = -(-(depth + 1) // unroll) * unroll

    def step(i, r, known):
        for lag, stage in stages:
            if not known or 0 <= i - lag < count:
                stage(i - lag, (r - lag) % unroll, i - lag if known else unroll)
    if peeled >= count:
        peeled = count
    for i in range(peeled):
        step(i, i % unroll, True)
    if peeled < count:
        with eng.Fori(peeled // unroll, count // unroll) as m:
            if before:
                before(unroll * m)
            for r in range(unroll):
                step(unroll * m + r, r, False)
    for i in range(count, count + depth - 1):
        step(i, i % unroll, True)


def combine(nc, t, wo, bo, gate_w, gate_b, grp, load_more=None):
    h0, halves = 2 * grp.graph0, 2 * grp.graphs
    own = slice(QPH * h0, QPH * (h0 + halves))
    ctx = ExitStack()
    with ctx:
        sb = lambda name, shape, dt=F32: ctx.enter_context(nc.sbuf_tensor(name + grp.tag, shape, dt))
        ps = lambda name, shape, dt=F32: ctx.enter_context(nc.psum_tensor(name + grp.tag, shape, dt))
        sem = stage_semaphores(nc, ctx, grp.tag)
        two = lambda name: [sem(f"{name}{p}") for p in range(2)]
        pair = lambda name, shape, dt=F32: [sb(f"{name}{p}", shape, dt) for p in range(2)]
        wo_sb, gw_sb = sb("wo_sb", [P, D]), sb("gw_sb", [P, E])
        bo_row, gb_row = sb("bo_row", [P, D]), sb("gb_row", [P, E])
        raw = pair("raw", [P, GROUPS, HALF])
        rsum = pair("rsum", [P, QPH * H])
        cn = pair("cn", [P, QPH * H, HD])
        cnT = pair("cnT", [P, HALF])
        stats, meanvar = pair("stats_", [P, QPH, 6]), pair("meanvar_", [P, QPH, 2])
        vareps, std, rstd = pair("vareps_", [P, QPH]), pair("std_", [P, QPH]), pair("rstd_", [P, QPH])
        xn = pair("xn_", [P, QPH, D])
        xnT = pair("xnT_", [P, HALF])
        logits = pair("logits", [P, QPH, E])
        best, best_index = pair("best", [P, QPH, 8]), pair("best_index", [P, QPH, 8], mybir.dt.uint32)
        kept, xn_kept = two("kept"), sem("xn_kept")
        a_ps = ps("a_ps", [P, QPH, GROUPS, P])
        b_ps, c_ps = ps("b_ps", [P, QPH, P]), ps("c_ps", [P, QPH, P])
        y_ps = [ps(f"proj_ps{p}", [P, QPH, D]) for p in range(2)]
        l_ps = ps("l_ps", [P, QPH, E])
        raw_loaded, c_loaded = two("raw_loaded"), sem("c_loaded")
        xb_done = two("xb_done")
        a_done, rsum_done, cn_done = sem("a_done"), sem("rsum_done"), sem("cn_done")
        b_done, cnT_done, y_done, x2_done = sem("b_done"), sem("cnT_done"), sem("y_done"), sem("x2_done")
        stat_done, aggr_done, vareps_done = sem("stat_done_"), sem("aggr_done_"), sem("vareps_done_")
        std_done, rstd_done, xn_done = sem("std_done_"), sem("rstd_done_"), sem("xn_done_")
        c_done, xnT_done, l_done, logit_done = sem("c_done"), sem("xnT_done_"), sem("l_done"), sem("logit_done")
        top_done, index_done = sem("top_done"), sem("index_done")
        gate_step = sem("gate_step")
        block = ctx.enter_context(nc.Block())

        @block.sync
        def _(sp):
            sp.dma_start(wo_sb[:, :], wo).then_inc(c_loaded, 16)
            sp.dma_start(gw_sb[:, :], gate_w).then_inc(c_loaded, 16)
            sp.dma_start(bo_row[:, :], bo.partition_broadcast(P)).then_inc(c_loaded, 16)
            sp.dma_start(gb_row[:, :], gate_b.partition_broadcast(P)).then_inc(c_loaded, 16)

            def load_raw(n, p, early):
                if early > 1:
                    sp.wait_ge(a_done, n - 1)
                sp.dma_start(raw[p][:, :, :], t.ctx_dram[h0 + n].rearrange("g p q -> p g q")).then_inc(raw_loaded[p], 16)

            staggered(sp, halves, ((0, load_raw),))
            if load_more:
                load_more(sp)

        @block.gpsimd
        def _(pool):
            pool.wait_ge(c_loaded, 64)

            def add_bias(n, p, early):
                for q in range(QPH):
                    tile = t.x2[:, QPH * (h0 + n) + q, :]
                    nc.gpsimd.tensor_tensor(tile, tile, bo_row[:, :], ALU.add).then_inc(xb_done[p], 1)

            def keep(n, p, early):
                pool.wait_ge(xn_done, QPH * n + QPH)
                nc.gpsimd.tensor_copy(t.xn2[:, bass.ds(QPH * (h0 + n), QPH), :], xn[p][:, :, :]).then_inc(xn_kept, 1)

            staggered(pool, halves, ((1, add_bias), (2, keep)))

        @block.tensor
        def _(pe):
            pe.wait_ge(c_loaded, 64)

            def heads(n, p, early):
                pe.wait_ge(raw_loaded[p], 8 * (n - p) + 16)
                if early > 0:
                    pe.wait_ge(cn_done, n)
                for q in range(QPH):
                    for g in range(GROUPS):
                        last = nc.tensor.transpose(a_ps[:, q, g, :], raw[p][:, g, q * P:(q + 1) * P], t.ident[:, :])
                last.then_inc(a_done, 1)

            def turn_back(n, p, early):
                pe.wait_ge(cn_done, n + 1)
                if early > 0:
                    pe.wait_ge(cnT_done, n)
                for q in range(QPH):
                    src = cn[p][:, q * H:(q + 1) * H, :].rearrange("p h d -> p (h d)")
                    last = nc.tensor.transpose(b_ps[:, q, :], src, t.ident[:, :])
                last.then_inc(b_done, 1)

            def project(n, p, early):
                pe.wait_ge(cnT_done, n + 1)
                if early > 1:
                    pe.wait_ge(x2_done, n - 1)
                for q in range(QPH):
                    last = nc.tensor.matmul(y_ps[p][:, q, :], cnT[p][:, q * P:(q + 1) * P], wo_sb[:, :],
                                            start=True, stop=True)
                last.then_inc(y_done, 1)

            def turn_norm(n, p, early):
                pe.wait_ge(xn_done, QPH * n + QPH)
                if early > 0:
                    pe.wait_ge(xnT_done, n)
                for q in range(QPH):
                    last = nc.tensor.transpose(c_ps[:, q, :], xn[p][:, q, :], t.ident[:, :])
                last.then_inc(c_done, 1)

            def route(n, p, early):
                pe.wait_ge(xnT_done, n + 1)
                if early > 0:
                    pe.wait_ge(logit_done, n)
                for q in range(QPH):
                    last = nc.tensor.matmul(l_ps[:, q, :], xnT[p][:, q * P:(q + 1) * P], gw_sb[:, :],
                                            start=True, stop=True)
                last.then_inc(l_done, 1)

            staggered(pe, halves, ((1, turn_back), (3, turn_norm), (0, heads), (1, project), (3, route)))

        @block.scalar
        def _(act):
            def copy_heads(n, p, early):
                act.wait_ge(b_done, n + 1)
                if early > 1:
                    act.wait_ge(y_done, n - 1)
                nc.scalar.activation(cnT[p][:, :], b_ps[:, :, :].rearrange("p q d -> p (q d)"), ACT.Copy)\
                    .then_inc(cnT_done, 1)

            def deviation(n, p, early):
                act.wait_ge(vareps_done, n + 1)
                nc.scalar.activation(std[p][:, :], vareps[p][:, :], ACT.Sqrt).then_inc(std_done, 1)

            def copy_norm(n, p, early):
                act.wait_ge(c_done, n + 1)
                if early > 1:
                    act.wait_ge(l_done, n - 1)
                nc.scalar.activation(xnT[p][:, :], c_ps[:, :, :].rearrange("p q d -> p (q d)"), ACT.Copy)\
                    .then_inc(xnT_done, 1)

            staggered(act, halves, ((1, copy_heads), (3, copy_norm), (2, deviation)))
            act.wait_ge(gate_step, 1)
            nc.scalar.activation(t.gate[:, own, 1], t.gate_gap[:, own], ACT.Exp).then_inc(gate_step, 1)

        @block.vector
        def _(dve):
            def divide(n, p, early):
                dve.wait_ge(a_done, n + 1)
                a = a_ps[:, :, :, :].rearrange("p q g (j w) -> p (q g j) w", w=VW)
                nc.vector.reciprocal(rsum[p][:, :], a[:, :, HD]).then_inc(rsum_done, 1)
                dve.wait_ge(rsum_done, n + 1)
                if early > 1:
                    dve.wait_ge(b_done, n - 1)
                nc.vector.tensor_tensor(cn[p][:, :, :], a[:, :, 0:HD],
                                        rsum[p][:, :].unsqueeze(2).broadcast_to([P, QPH * H, HD]), ALU.mult)\
                    .then_inc(cn_done, 1)

            def statistics(n, p, early):
                dve.wait_ge(y_done, n + 1)
                dve.wait_ge(xb_done[p], QPH // 2 * (n - p) + QPH)
                own_x = t.x2[:, bass.ds(QPH * (h0 + n), QPH), :]
                nc.vector.tensor_tensor(own_x, y_ps[p][:, :, :], own_x, ALU.add).then_inc(x2_done, 1)
                dve.wait_ge(x2_done, n + 1)
                for q in range(QPH):
                    nc.vector.bn_stats(stats[p][:, q, :], t.x2[:, QPH * (h0 + n) + q, :]).then_inc(stat_done, 1)
                dve.wait_ge(stat_done, QPH * n + QPH)
                t.alone(dve)
                for q in range(QPH):
                    nc.vector.bn_aggr(meanvar[p][:, q, :], stats[p][:, q, :]).then_inc(aggr_done, 1)
                dve.wait_ge(aggr_done, QPH * n + QPH)
                nc.vector.tensor_scalar(vareps[p][:, :], meanvar[p][:, :, 1], EPS, None, ALU.add)\
                    .then_inc(vareps_done, 1)

            def normalise(n, p, early):
                dve.wait_ge(std_done, n + 1)
                nc.vector.reciprocal(rstd[p][:, :], std[p][:, :]).then_inc(rstd_done, 1)
                dve.wait_ge(rstd_done, n + 1)
                if early > 1:
                    dve.wait_ge(c_done, n - 1)
                    dve.wait_ge(xn_kept, n - 1)
                for q in range(QPH):
                    nc.vector.tensor_scalar(xn[p][:, q, :], t.x2[:, QPH * (h0 + n) + q, :], meanvar[p][:, q, 0:1],
                                            rstd[p][:, q:q + 1], ALU.subtract, ALU.mult).then_inc(xn_done, 1)

            def choose(n, p, early):
                dve.wait_ge(l_done, n + 1)
                if early > 1:
                    dve.wait_ge(kept[p], n - p)
                nc.vector.tensor_tensor(logits[p][:, :, :], l_ps[:, :, :],
                                        gb_row[:, :].unsqueeze(1).broadcast_to([P, QPH, E]), ALU.add)\
                    .then_inc(logit_done, 1)
                dve.wait_ge(logit_done, n + 1)
                t.alone(dve)
                for q in range(QPH):
                    nc.vector.max(best[p][:, q, :], logits[p][:, q, :]).then_inc(top_done, 1)
                dve.wait_ge(top_done, QPH * n + QPH)
                t.alone(dve)
                for q in range(QPH):
                    nc.vector.max_index(best_index[p][:, q, :], best[p][:, q, :], logits[p][:, q, :])\
                        .then_inc(index_done, 1)
                dve.wait_ge(index_done, QPH * n + QPH)
                nc.vector.tensor_copy(t.top[:, bass.ds(QPH * (h0 + n), QPH), :], best[p][:, :, 0:2]).then_inc(kept[p], 1)
                nc.vector.tensor_copy(t.top_index[:, bass.ds(QPH * (h0 + n), QPH), :], best_index[p][:, :, 0:2])\
                    .then_inc(kept[p], 1)

            dve.wait_ge(c_loaded, 64)
            staggered(dve, halves, ((4, choose), (2, statistics), (0, divide), (2, normalise)))
            for p in range(2):
                dve.wait_ge(kept[p], halves)
            nc.vector.tensor_tensor(t.gate_gap[:, own], t.top[:, own, 1], t.top[:, own, 0], ALU.subtract).then_inc(gate_step, 1)
            dve.wait_ge(gate_step, 2)
            nc.vector.tensor_scalar(t.gate_sum[:, own], t.gate[:, own, 1], 1.0, None, ALU.add).then_inc(gate_step, 1)
            dve.wait_ge(gate_step, 3)
            nc.vector.reciprocal(t.gate[:, own, 0], t.gate_sum[:, own]).then_inc(gate_step, 1)
            dve.wait_ge(gate_step, 4)
            nc.vector.tensor_tensor(t.gate[:, own, 1], t.gate[:, own, 1], t.gate[:, own, 0], ALU.mult).then_inc(gate_step, 1)
            dve.wait_ge(gate_step, 5)


def route(nc, t, grp):
    nt, slots = grp.tiles, grp.slot_tiles
    own = slice(grp.tile0, grp.tile0 + nt)
    ctx = ExitStack()
    with ctx:
        sb = lambda name, shape, dt=F32: ctx.enter_context(nc.sbuf_tensor(name + grp.tag, shape, dt))
        sem = stage_semaphores(nc, ctx, grp.tag)
        before, ones = sb("before", [P, P], BF16), sb("ones", [P, P], BF16)
        scan_ones = sb("scan_ones", [P, E * nt])
        chosen = [sb(f"chosen{j}", [P, nt, E], BF16) for j in range(2)]
        either = sb("either", [P, nt, E], BF16)
        count = sb("count", [P, E, nt])
        upto = sb("upto", [P, E, nt])
        offset = sb("offset", [P, E, nt])
        total, total_int = sb("total", [P, E]), sb("total_int", [P, E], I32)
        etiles, tile_end, slot_base = sb("etiles", [P, E]), sb("tile_end", [P, E]), sb("slot_base", [P, E])
        row = sb("row", [P, nt, E])
        picked = [sb(f"picked{j}", [P, nt, E]) for j in range(2)]
        slot32 = [sb(f"slot32{j}", [P, nt]) for j in range(2)]
        iota_e, iota_s = sb("iota_e", [P, E]), sb("iota_s", [P, slots])
        passed, expert32 = sb("passed", [1, slots, E]), sb("expert32", [1, slots])
        rank_ps = ctx.enter_context(nc.psum_tensor("rank_ps" + grp.tag, [P, 2, 512], F32))
        count_ps = ctx.enter_context(nc.psum_tensor("count_ps" + grp.tag, [P, 2, 512], F32))
        pool_step, pe_done, step = sem("pool_step"), sem("pe_done"), sem("route_step")
        hb = nt // 2
        assert hb * E <= 512
        block = ctx.enter_context(nc.Block())

        @block.gpsimd
        def _(pool):
            nc.gpsimd.memset(before[:, :], 1.0).then_inc(pool_step, 1)
            nc.gpsimd.memset(ones[:, :], 1.0).then_inc(pool_step, 1)
            nc.gpsimd.iota(iota_e[:, :], [[1, E]], base=0, channel_multiplier=0,
                           allow_small_or_imprecise_dtypes=True).then_inc(pool_step, 1)
            nc.gpsimd.iota(iota_s[:, :], [[1, slots]], base=0, channel_multiplier=0,
                           allow_small_or_imprecise_dtypes=True).then_inc(pool_step, 1)
            pool.wait_ge(pool_step, 4)
            nc.gpsimd.affine_select(out=before[:, :], in_=before[:, :], compare_op=ALU.is_gt, fill=0.0,
                                    base=0, pattern=[[1, P]], channel_multiplier=-1).then_inc(pool_step, 1)

        @block.tensor
        def _(pe):
            pe.wait_ge(pool_step, 5)
            pe.wait_ge(step, 3)
            for lhs, out in ((before, rank_ps), (ones, count_ps)):
                for c in range(2):
                    last = nc.tensor.matmul(out[:, c, 0:hb * E], lhs[:, :],
                                            either[:, c * hb:(c + 1) * hb, :].rearrange("p t e -> p (t e)"),
                                            start=True, stop=True)
            last.then_inc(pe_done, 1)

        @block.vector
        def _(dve):
            steps = [0]

            def then(ins):
                steps[0] += 1
                ins.then_inc(step, 1)
                dve.wait_ge(step, steps[0])

            dve.wait_ge(pool_step, 5)
            for j in range(2):
                then(nc.vector.tensor_tensor(chosen[j][:, :, :], iota_e[:, :].unsqueeze(1).broadcast_to([P, nt, E]),
                                             t.top_index[:, own, j].unsqueeze(2).broadcast_to([P, nt, E]), ALU.is_equal))
            then(nc.vector.tensor_tensor(either[:, :, :], chosen[0][:, :, :], chosen[1][:, :, :], ALU.add))
            then(nc.vector.memset(scan_ones[:, :], 1.0))
            dve.wait_ge(pe_done, 1)
            bank = lambda ps, c: ps[:, c, 0:hb * E].rearrange("p (t e) -> p t e", e=E)
            for c in range(2):
                then(nc.vector.tensor_copy(count[:, :, c * hb:(c + 1) * hb], bank(count_ps, c).rearrange("p t e -> p e t")))
            flat = lambda a: a[:, :, :].rearrange("p e t -> p (e t)")
            then(nc.vector.tensor_tensor_scan(flat(upto), scan_ones[:, :], flat(count), 0.0, ALU.mult, ALU.add))
            then(nc.vector.tensor_tensor(flat(offset), flat(upto), flat(count), ALU.subtract))
            then(nc.vector.tensor_tensor(total[:, :], upto[:, :, nt - 1], offset[:, :, 0], ALU.subtract))
            then(nc.vector.tensor_scalar(total_int[:, :], total[:, :], float(P - 1), None, ALU.add))
            then(nc.vector.tensor_scalar(total_int[:, :], total_int[:, :], 7, None, ALU.logical_shift_right))
            then(nc.vector.tensor_copy(etiles[:, :], total_int[:, :]))
            then(nc.vector.tensor_tensor_scan(tile_end[:, :], scan_ones[:, 0:E], etiles[:, :], 0.0, ALU.mult, ALU.add))
            then(nc.vector.tensor_tensor(slot_base[:, :], tile_end[:, :], etiles[:, :], ALU.subtract))
            then(nc.vector.scalar_tensor_tensor(out=slot_base[:, :], in0=slot_base[:, :], scalar=float(P),
                                                in1=offset[:, :, 0], op0=ALU.mult, op1=ALU.subtract))
            then(nc.vector.tensor_tensor(offset[:, :, :], offset[:, :, :],
                                         slot_base[:, :].unsqueeze(2).broadcast_to([P, E, nt]), ALU.add))
            for c in range(2):
                tt = slice(c * hb, (c + 1) * hb)
                then(nc.vector.tensor_tensor(row[:, tt, :], bank(rank_ps, c), offset[:, :, tt].rearrange("p e t -> p t e"),
                                             ALU.add))
            for j in range(2):
                then(nc.vector.tensor_tensor(picked[j][:, :, :], row[:, :, :], chosen[j][:, :, :], ALU.mult))
                then(nc.vector.tensor_reduce(slot32[j][:, :], picked[j][:, :, :], mybir.AxisListType.X, ALU.add))
                then(nc.vector.tensor_copy(t.slot[:, own, j], slot32[j][:, :]))
            then(nc.vector.tensor_tensor(passed[:, :, :], tile_end[0:1, :].unsqueeze(1).broadcast_to([1, slots, E]),
                                         iota_s[0:1, :].unsqueeze(2).broadcast_to([1, slots, E]), ALU.is_le))
            then(nc.vector.tensor_reduce(expert32[:, :], passed[:, :, :], mybir.AxisListType.X, ALU.add))
            then(nc.vector.tensor_scalar(grp.expert[:, :], expert32[:, :], float(E - 1), None, ALU.min))


class Scatter:

    def __init__(self, nc, ctx, t, grp):
        self.t, self.grp = t, grp
        self.done = ctx.enter_context(nc.semaphore("scattered" + grp.tag))
        self.rows = [(tile, j) for tile in range(grp.tile0, grp.tile0 + grp.tiles) for j in range(2)]

    def run(self, pool, a, b):
        pool.wait_ge(self.t.zeroed, 32)
        for tile, j in self.rows[a:b]:
            pool.indirect_dma_start(self.grp.xs_dram[:, :],
                                    bass.IndirectOffsetOnAxis(ap=self.t.slot[:, tile, j:j + 1], axis=0),
                                    self.t.xn2[:, tile, :], None).then_inc(self.done, 16)

    def wait(self, pool):
        pool.wait_ge(self.done, 16 * len(self.rows))


class Gather:

    def __init__(self, nc, ctx, t, grp, chunk=4):
        self.t, self.grp, self.chunk = t, grp, chunk
        self.done = [ctx.enter_context(nc.semaphore(f"gathered{c}" + grp.tag)) for c in range(grp.tiles // chunk)]

    def run(self, pool):
        for i in range(self.grp.tiles):
            tile = self.grp.tile0 + i
            for j in range(2):
                pool.indirect_dma_start(self.t.y[:, tile, j, :], None, self.grp.ys_dram[:, :],
                                        bass.IndirectOffsetOnAxis(ap=self.t.slot[:, tile, j:j + 1], axis=0))\
                    .then_inc(self.done[i // self.chunk], 16)


def experts(nc, t, grp, pool_work):
    rows = lambda dram: dram.rearrange("(t p) d -> t p d", p=P)
    KH = HID // P
    XRING = 8
    UP, DOWN = 1, 3
    slots = grp.slot_tiles
    ctx = ExitStack()
    with ctx:
        sb = lambda name, shape, dt=F32: ctx.enter_context(nc.sbuf_tensor(name + grp.tag, shape, dt))
        ps = lambda name, shape, dt=F32: ctx.enter_context(nc.psum_tensor(name + grp.tag, shape, dt))
        sem = stage_semaphores(nc, ctx, grp.tag)
        two = lambda name: [sem(f"{name}{p}") for p in range(2)]
        pair = lambda name, shape, dt=F32: [sb(f"{name}{p}", shape, dt) for p in range(2)]
        x_in, xT = [sb(f"x_in{r}", [P, D]) for r in range(XRING)], pair("xT", [P, P])
        silu, hidden, hT = pair("silu", [P, HID]), pair("hidden", [P, HID]), pair("hT", [P, HID])
        y = pair("y", [P, D])
        x_ps = ps("x_ps", [P, P])
        h_ps = [ps(f"h_ps{p}", [P, 2 * HID]) for p in range(2)]
        t_ps = [ps(f"t_ps{p}", [P, HID]) for p in range(2)]
        y_ps = [ps(f"y_ps{p}", [P, D]) for p in range(2)]
        x_loaded = [sem(f"x_loaded{r}") for r in range(XRING)]
        x_turned, xT_done = sem("x_turned"), sem("xT_done")
        h_done, silu_done, hidden_done = sem("h_done"), sem("silu_done"), sem("hidden_done")
        turned, hT_done, y_done, y_copied = sem("turned"), sem("hT_done"), sem("y_done"), sem("y_copied")
        stored = two("stored")
        work = pool_work(ctx)
        block = ctx.enter_context(nc.Block())

        @block.sync
        def _(sp):
            def load(n, r, early):
                if early >= XRING:
                    sp.wait_ge(x_turned, n - XRING + 1)
                sp.dma_start(x_in[r][:, :], rows(grp.xs_dram)[n]).then_inc(x_loaded[r], 16)

            def store(n, r, early):
                p = r % 2
                sp.wait_ge(y_copied, n + 1)
                sp.dma_start(rows(grp.ys_dram)[n], y[p][:, :]).then_inc(stored[p], 16)

            staggered(sp, slots, ((0, load), (5, store)), XRING)
            for p in range(2):
                sp.wait_ge(stored[p], 16 * (slots // 2))

        @block.gpsimd
        def _(pool):
            work(pool)

        @block.tensor
        def _(pe):
            numbers = {}

            def load_experts(i):
                least = i - DOWN
                _, values = nc.values_load_multi_w_load_instructions(
                    grp.expert[0:1, bass.ds(least, XRING + DOWN - UP)], engines=(mybir.EngineType.PE,),
                    min_val=0, max_val=E - 1,
                    skip_runtime_bounds_check_because="route() takes the least of its count and the last expert")
                numbers.clear()
                numbers.update({k - DOWN: value for k, value in enumerate(values)})

            def expert_of(n, r, stage):
                if isinstance(n, int):
                    return pe.value_load(grp.expert[0:1, n:n + 1], min_val=0, max_val=E - 1)
                return numbers[(r + stage) % XRING - stage]

            def turn_x(n, r, early):
                pe.wait_ge(x_loaded[r], 16 // XRING * (n - r) + 16)
                if early > 0:
                    pe.wait_ge(xT_done, n)
                nc.tensor.transpose(x_ps[:, :], x_in[r][:, :], t.ident[:, :]).then_inc(x_turned, 1)

            def up(n, r, early):
                p, e = r % 2, expert_of(n, r, UP)
                pe.wait_ge(xT_done, n + 1)
                if early > 1:
                    pe.wait_ge(hidden_done, n - 1)
                nc.tensor.matmul(h_ps[p][:, :], xT[p][:, :], t.w12[:, e, :], start=True, stop=True)\
                    .then_inc(h_done, 1)

            def turn_hidden(n, r, early):
                p = r % 2
                pe.wait_ge(hidden_done, n + 1)
                if early > 1:
                    pe.wait_ge(hT_done, n - 1)
                for k in range(KH):
                    last = nc.tensor.transpose(t_ps[p][:, k * P:(k + 1) * P], hidden[p][:, k * P:(k + 1) * P],
                                               t.ident[:, :])
                last.then_inc(turned, 1)

            def down(n, r, early):
                p, e = r % 2, expert_of(n, r, DOWN)
                pe.wait_ge(hT_done, n + 1)
                if early > 1:
                    pe.wait_ge(y_copied, n - 1)
                for k in range(KH):
                    last = nc.tensor.matmul(y_ps[p][:, :], hT[p][:, k * P:(k + 1) * P], t.w3[:, e, k, :],
                                            start=(k == 0), stop=(k == KH - 1))
                last.then_inc(y_done, 1)

            pe.wait_ge(t.weights_loaded, 16 * (2 + KH))
            staggered(pe, slots, ((UP, up), (0, turn_x), (DOWN, down), (2, turn_hidden)), XRING, load_experts)

        @block.scalar
        def _(act):
            def copy_x(n, r, early):
                p = r % 2
                act.wait_ge(x_turned, n + 1)
                if early > 1:
                    act.wait_ge(h_done, n - 1)
                nc.scalar.activation(xT[p][:, :], x_ps[:, :], ACT.Copy).then_inc(xT_done, 1)

            def gate_up(n, r, early):
                p = r % 2
                act.wait_ge(h_done, n + 1)
                if early > 1:
                    act.wait_ge(hidden_done, n - 1)
                nc.scalar.activation(silu[p][:, :], h_ps[p][:, 0:HID], ACT.Silu).then_inc(silu_done, 1)

            def copy_hidden(n, r, early):
                p = r % 2
                act.wait_ge(turned, n + 1)
                if early > 1:
                    act.wait_ge(y_done, n - 1)
                nc.scalar.activation(hT[p][:, :], t_ps[p][:, :], ACT.Copy).then_inc(hT_done, 1)

            staggered(act, slots, ((0, copy_x), (1, gate_up), (2, copy_hidden)), XRING)

        @block.vector
        def _(dve):
            def multiply(n, r, early):
                p = r % 2
                dve.wait_ge(silu_done, n + 1)
                if early > 1:
                    dve.wait_ge(turned, n - 1)
                nc.vector.tensor_tensor(hidden[p][:, :], h_ps[p][:, HID:], silu[p][:, :], ALU.mult)\
                    .then_inc(hidden_done, 1)

            def copy_y(n, r, early):
                p = r % 2
                dve.wait_ge(y_done, n + 1)
                if early > 1:
                    dve.wait_ge(stored[p], 8 * (n - p))
                nc.vector.tensor_copy(y[p][:, :], y_ps[p][:, :]).then_inc(y_copied, 1)

            staggered(dve, slots, ((1, multiply), (3, copy_y)), XRING)


def finish(nc, t, groups, out, gathers):
    chunk = gathers[0].chunk
    out_v = out.rearrange("b (t p) d -> p (b t) d", p=P)
    chunks = [(g, c) for g in range(len(groups)) for c in range(groups[g].tiles // chunk)]
    ctx = ExitStack()
    with ctx:
        scaled, summed = ctx.enter_context(nc.semaphore("scaled")), ctx.enter_context(nc.semaphore("summed"))
        stored = ctx.enter_context(nc.semaphore("out_stored"))
        block = ctx.enter_context(nc.Block())

        @block.gpsimd
        def _(pool):
            gathers[1].run(pool)

        @block.vector
        def _(dve):
            n = 0
            for g, c in chunks:
                dve.wait_ge(gathers[g].done[c], 32 * chunk)
                for j in range(2):
                    for q in range(chunk):
                        tile = groups[g].tile0 + c * chunk + q
                        if j == 1:
                            dve.wait_ge(scaled, n * chunk + q + 1)
                        nc.vector.scalar_tensor_tensor(out=t.x2[:, tile, :], in0=t.y[:, tile, j, :],
                                                       scalar=t.gate[:, tile, j:j + 1], in1=t.x2[:, tile, :],
                                                       op0=ALU.mult, op1=ALU.add).then_inc((scaled, summed)[j], 1)
                n += 1

        @block.sync
        def _(sp):
            for n, (g, c) in enumerate(chunks):
                sp.wait_ge(summed, (n + 1) * chunk)
                tile = groups[g].tile0 + c * chunk
                sp.dma_start(out_v[:, tile:tile + chunk, :], t.x2[:, tile:tile + chunk, :]).then_inc(stored, 16)
            sp.wait_ge(stored, 16 * len(chunks))


class Group:

    def __init__(self, nc, ctx, k, graph0, graphs):
        self.tag = f"_{k}"
        self.graph0, self.graphs = graph0, graphs
        self.tile0, self.tiles = graph0 * TPB, graphs * TPB
        self.slot_tiles = (2 * self.tiles + E - 1 + 7) // 8 * 8
        self.xs_dram = nc.dram_tensor(f"xs_dram{k}", (self.slot_tiles * P, D), F32, kind="Internal").ap()
        self.ys_dram = nc.dram_tensor(f"ys_dram{k}", (self.slot_tiles * P, D), F32, kind="Internal").ap()
        self.expert = ctx.enter_context(nc.sbuf_tensor(f"expert{k}", [1, self.slot_tiles], I32))


def load_weights(sp, t, w1, w2, w3):
    sp.dma_start(t.w12[:, :, 0:HID], w1.rearrange("e d h -> d e h")).then_inc(t.weights_loaded, 16)
    sp.dma_start(t.w12[:, :, HID:], w2.rearrange("e d h -> d e h")).then_inc(t.weights_loaded, 16)
    for k in range(HID // P):
        sp.dma_start(t.w3[:, :, k, :], w3.rearrange("e (k p) d -> k p e d", p=P)[k]).then_inc(t.weights_loaded, 16)


class Shared:

    CONSTS = 4

    def alone(self, eng):
        eng.sem_inc(self.waits_carried, 1)


def program(nc, x, adj, wq, wk, wv, wo, bo, gate_w, gate_b, w1, w2, w3, out):
    t = Shared()
    ctx = ExitStack()
    with ctx:
        sb = lambda name, shape, dt=F32: ctx.enter_context(nc.sbuf_tensor(name, shape, dt))
        t.ident, t.identb = sb("ident", [P, P]), sb("identb", [P, P], BF16)
        t.top, t.top_index = sb("top", [P, TILES, 2]), sb("top_index", [P, TILES, 2])
        t.gate, t.gate_gap, t.gate_sum = sb("gate", [P, TILES, 2]), sb("gate_gap", [P, TILES]), sb("gate_sum", [P, TILES])
        t.zeros = sb("zeros", [P, ZEROS])
        t.zeroed = ctx.enter_context(nc.semaphore("zeroed"))
        t.consts_done = ctx.enter_context(nc.semaphore("consts_done"))
        t.waits_carried = ctx.enter_context(nc.semaphore("waits_carried"))
        t.parts_dram = nc.dram_tensor("parts_dram", (B, 2, 3, P, N), BF16, kind="Internal").ap()
        t.v_dram = nc.dram_tensor("v_dram", (B, N, H * VW), F32, kind="Internal").ap()
        t.ctx_dram = nc.dram_tensor("ctx_dram", (HALVES, GROUPS, P, HALF), F32, kind="Internal").ap()
        t.x2, t.xn2 = sb("x2", [P, TILES, D]), sb("xn2", [P, TILES, D])
        t.slot = sb("slot", [P, TILES, 2], mybir.dt.uint32)
        groups = [Group(nc, ctx, 0, 0, SPLIT), Group(nc, ctx, 1, SPLIT, B - SPLIT)]
        with nc.Block() as block:
            @block.gpsimd
            def _(pool):
                nc.gpsimd.memset(t.ident[:, :], 0.0).then_inc(t.consts_done, 1)
                pool.wait_ge(t.consts_done, 1)
                nc.gpsimd.affine_select(out=t.ident[:, :], in_=t.ident[:, :], compare_op=ALU.not_equal, fill=1.0,
                                        base=0, pattern=[[-1, P]], channel_multiplier=1).then_inc(t.consts_done, 1)
                pool.wait_ge(t.consts_done, 2)
                nc.gpsimd.tensor_copy(t.identb[:, :], t.ident[:, :]).then_inc(t.consts_done, 1)
                nc.gpsimd.memset(t.zeros[:, :], 0.0).then_inc(t.consts_done, 1)
        prepare(nc, t, x, wq, wk, wv)
        attention(nc, t, adj, groups[0], None, fill=groups)
        combine(nc, t, wo, bo, gate_w, gate_b, groups[0])
        route(nc, t, groups[0])
        attention(nc, t, adj, groups[1], Scatter(nc, ctx, t, groups[0]))
        t.w12 = sb("w12", [P, E, 2 * HID])
        t.w3 = sb("w3", [P, E, HID // P, D])
        t.weights_loaded = ctx.enter_context(nc.semaphore("weights_loaded"))
        combine(nc, t, wo, bo, gate_w, gate_b, groups[1], lambda sp: load_weights(sp, t, w1, w2, w3))
        route(nc, t, groups[1])
        t.y = sb("y_rows", [P, TILES, 2, D])
        scatter = Scatter(nc, ctx, t, groups[1])

        def send(_):
            def work(pool):
                scatter.run(pool, 0, len(scatter.rows))
                scatter.wait(pool)
            return work
        experts(nc, t, groups[0], send)
        gathers = [Gather(nc, ctx, t, g) for g in groups]
        experts(nc, t, groups[1], lambda _: gathers[0].run)
        finish(nc, t, groups, out, gathers)


_INS = ["x", "adj", "L0_gnn_Wq", "L0_gnn_Wk", "L0_gnn_Wv", "L0_gnn_Wo", "L0_gnn_bo", "L0_ffn_gate_w", "L0_ffn_gate_b",
        "L0_ffn_w1", "L0_ffn_w2", "L0_ffn_w3"]
_OUTS = [((B, N, D), "float32")]


def kernel(**inputs):
    import numpy as _np
    import concourse.bacc as _bacc
    from concourse import mybir as _mybir
    from concourse.bass_utils import run_bass_kernel_spmd as _run

    nc = _bacc.Bacc("TRN2", target_bir_lowering=False, num_devices=1)
    nc.disable_value_cache = True
    arrays, args = {}, []
    for name in _INS:
        a = _np.ascontiguousarray(inputs[name])
        arrays[f"in_{name}_dram"] = a
        args.append(nc.dram_tensor(f"in_{name}_dram", a.shape, _mybir.dt.from_np(a.dtype), kind="ExternalInput").ap())
    for i, (shape, dtype) in enumerate(_OUTS):
        dt = _mybir.dt.from_np(_np.dtype(dtype))
        args.append(nc.dram_tensor(f"out_{i}_dram", shape, dt, kind="ExternalOutput").ap())
    program(nc, *args)
    r = _run(nc, [arrays], core_ids=[0])
    got = tuple(r.results[0][f"out_{i}_dram"] for i in range(len(_OUTS)))
    return got[0]
```
